# Optimizing a Trainium2 kernel written in Bass

```python
import numpy as np
import jax
import jax.numpy as jnp

def _softmax(x, axis=-1):
    return jax.nn.softmax(x, axis=axis)

def _gelu(x):
    return jax.nn.gelu(x, approximate=True)

def _silu(x):
    return jax.nn.silu(x)

def _sigmoid(x):
    return jax.nn.sigmoid(x)

def _layernorm(x, axis=-1, eps=1e-05):
    m = jnp.mean(x, axis=axis, keepdims=True)
    v = jnp.var(x, axis=axis, keepdims=True)
    return (x - m) / jnp.sqrt(v + eps)

def _scatter_add(tgt, idx, src, axis=0):
    return tgt.at[idx].add(src)

def _segment_sum(src, seg, n):
    return jax.ops.segment_sum(src, seg, n)
kernel_name = 'mk_gnn_resnorm_d2_gnn_r8_2fa5d0'

def setup_inputs(seed: int=0):
    np.random.seed(seed)
    _w = jnp.asarray

    def _rec_inputs():
        import jax
        import jax.numpy as jnp
        _gk = jax.random.key(seed)
        x = -0.000202 + 1 * jax.random.normal(jax.random.fold_in(_gk, 1), (12500, 128), jnp.float32)
        src = jax.random.randint(jax.random.fold_in(_gk, 2), (400000,), 0, 12500, jnp.int32)
        dst = jax.random.randint(jax.random.fold_in(_gk, 3), (400000,), 0, 12500, jnp.int32)
        _o = jnp.argsort(dst, stable=True)
        src = src[_o]
        dst = dst[_o]
        edge_attr_64 = jax.random.uniform(jax.random.fold_in(_gk, 11), (400000, 64), jnp.float32, 0.0, 1)
        edge_weight = -0.000492943 + 0.999642 * jax.random.normal(jax.random.fold_in(_gk, 13), (400000,), jnp.float32)
        return (x, src, dst, edge_attr_64, edge_weight)
    x, src, dst, edge_attr_64, edge_weight = _rec_inputs()

    def _L0_gnn_setup():
        import jax, jax.numpy as jnp
        import numpy as np
        N_NODES = 6250
        N_EDGES = 75000
        D_FEAT = 128
        key = jax.random.key(seed)
        k1, k2, k3 = jax.random.split(key, 3)
        x = jax.random.normal(k1, (N_NODES, D_FEAT), dtype=jnp.float32)
        edge_index = jax.random.randint(k2, (2, N_EDGES), 0, N_NODES, dtype=jnp.int64)
        line_graph_val = jax.random.normal(k3, (N_EDGES,), dtype=jnp.float32)
        return {'x': x, 'edge_index': edge_index, 'line_graph_val': line_graph_val}
    _L0_gnn_all = _L0_gnn_setup()
    _L0_gnn_in = {k: v for k, v in _L0_gnn_all.items() if k in ()}
    del _L0_gnn_all

    def _L1_gnn_setup():
        import jax, jax.numpy as jnp
        import numpy as np
        N_ATOMS = 6250
        N_PAIRS = 100000
        F = 128
        R = 64
        N_RES = 3
        key = jax.random.key(seed)
        ks = jax.random.split(key, 16)
        s = 1.0 / np.sqrt(F)
        inp = {'atomic_embedding': jax.random.normal(ks[0], (N_ATOMS, F), jnp.float32), 'f_ij': jax.random.uniform(ks[1], (N_PAIRS, R), jnp.float32), 'pair_indices': jax.random.randint(ks[2], (2, N_PAIRS), 0, N_ATOMS, jnp.int64) if jax.config.jax_enable_x64 else jax.random.randint(ks[2], (2, N_PAIRS), 0, N_ATOMS, jnp.int32), 'Wg': jax.random.normal(ks[3], (F, R), jnp.float32) / np.sqrt(R), 'Wi': jax.random.normal(ks[4], (F, F), jnp.float32) * s, 'bi': jnp.zeros((F,), jnp.float32), 'Wj': jax.random.normal(ks[5], (F, F), jnp.float32) * s, 'bj': jnp.zeros((F,), jnp.float32), 'Wv': jax.random.normal(ks[6], (F, F), jnp.float32) * s, 'bv': jnp.zeros((F,), jnp.float32), 'gate': jnp.ones((F,), jnp.float32), 'res_W1': jax.random.normal(ks[7], (N_RES, F, F), jnp.float32) * s, 'res_b1': jnp.zeros((N_RES, F), jnp.float32), 'res_W2': jax.random.normal(ks[8], (N_RES, F, F), jnp.float32) * s, 'res_b2': jnp.zeros((N_RES, F), jnp.float32)}
        return inp
    _L1_gnn_all = _L1_gnn_setup()
    _L1_gnn_in = {k: v for k, v in _L1_gnn_all.items() if k in ('Wg', 'Wi', 'bi', 'Wj', 'bj', 'Wv', 'bv', 'gate', 'res_W1', 'res_b1', 'res_W2', 'res_b2')}
    del _L1_gnn_all
    return {'x': x, 'src': src, 'dst': dst, 'edge_attr_64': edge_attr_64, 'edge_weight': edge_weight, 'L1_gnn_Wg': _L1_gnn_in['Wg'], 'L1_gnn_Wi': _L1_gnn_in['Wi'], 'L1_gnn_bi': _L1_gnn_in['bi'], 'L1_gnn_Wj': _L1_gnn_in['Wj'], 'L1_gnn_bj': _L1_gnn_in['bj'], 'L1_gnn_Wv': _L1_gnn_in['Wv'], 'L1_gnn_bv': _L1_gnn_in['bv'], 'L1_gnn_gate': _L1_gnn_in['gate'], 'L1_gnn_res_W1': _L1_gnn_in['res_W1'], 'L1_gnn_res_b1': _L1_gnn_in['res_b1'], 'L1_gnn_res_W2': _L1_gnn_in['res_W2'], 'L1_gnn_res_b2': _L1_gnn_in['res_b2']}

def reference(x, src, dst, edge_attr_64, edge_weight, L1_gnn_Wg, L1_gnn_Wi, L1_gnn_bi, L1_gnn_Wj, L1_gnn_bj, L1_gnn_Wv, L1_gnn_bv, L1_gnn_gate, L1_gnn_res_W1, L1_gnn_res_b1, L1_gnn_res_W2, L1_gnn_res_b2):
    import jax
    import jax.numpy as jnp

    def _L0_gnn_ref(x, edge_index, line_graph_val):
        import jax, jax.numpy as jnp
        import numpy as np
        N_NODES = 6250
        N_EDGES = 75000
        D_FEAT = 128
        src = edge_index[0]
        dst = edge_index[1]
        n = x.shape[0]
        deg = jax.ops.segment_sum(jnp.ones_like(src, dtype=x.dtype), dst, num_segments=n)
        deg_inv_sqrt = jnp.where(deg > 0, deg ** (-0.5), jnp.zeros_like(deg))
        norm = deg_inv_sqrt[src] * deg_inv_sqrt[dst]
        msg = norm[:, None] * x[src]
        out = jax.ops.segment_sum(msg, dst, num_segments=n)
        return jax.nn.relu(out)

    def _L1_gnn_ref(atomic_embedding, f_ij, pair_indices, Wg, Wi, bi, Wj, bj, Wv, bv, gate, res_W1, res_b1, res_W2, res_b2):
        import jax, jax.numpy as jnp
        import numpy as np
        N_ATOMS = 6250
        N_PAIRS = 100000
        F = 128
        R = 64
        N_RES = 3
        sp = jax.nn.softplus
        idx_i = pair_indices[0]
        idx_j = pair_indices[1]
        x = sp(atomic_embedding)
        g = f_ij @ Wg.T
        u = sp(x @ Wi.T + bi)
        msg = sp(x[idx_j] @ Wj.T + bj) * g
        u = u + jax.ops.segment_sum(msg, idx_i, num_segments=x.shape[0])
        for k in range(res_W1.shape[0]):
            h = sp(sp(u) @ res_W1[k].T + res_b1[k])
            u = u + h @ res_W2[k].T + res_b2[k]
        u = sp(u)
        return gate * x + u @ Wv.T + bv
    edge_index = jnp.stack([src, dst])
    x = _layernorm(x + _L0_gnn_ref(x, edge_index, edge_weight), axis=-1)
    x = _layernorm(x + _L1_gnn_ref(x, edge_attr_64, edge_index, L1_gnn_Wg, L1_gnn_Wi, L1_gnn_bi, L1_gnn_Wj, L1_gnn_bj, L1_gnn_Wv, L1_gnn_bv, L1_gnn_gate, L1_gnn_res_W1, L1_gnn_res_b1, L1_gnn_res_W2, L1_gnn_res_b2), axis=-1)
    return x

_drawn_inputs = setup_inputs


def setup_inputs(seed=0):
    import zlib

    import numpy as np

    out = dict(_drawn_inputs(seed))
    spreads = {'L1_gnn_bi': (0.0, 2.0),
     'L1_gnn_bj': (0.0, 0.1),
     'L1_gnn_bv': (0.0, 0.8),
     'L1_gnn_gate': (1.0, 0.6),
     'L1_gnn_res_b1': (0.0, 0.8),
     'L1_gnn_res_b2': (0.0, 0.723)}
    factors = {}
    for name, (base, spread) in spreads.items():
        noise = np.random.default_rng([zlib.crc32(name.encode()), seed]).standard_normal(out[name].shape)
        drawn = base * np.exp(spread * noise) if base else spread * noise
        out[name] = jnp.asarray(drawn.astype(out[name].dtype))
    for name, factor in factors.items():
        out[name] = (out[name] * factor).astype(out[name].dtype)
    return out
```

```python
from contextlib import ExitStack

import concourse.bass as bass
from concourse import mybir

P = 128
GT = 4
CG = 6
CT = GT * CG
GE = GT * P
CE = CT * P
ACCS = 8
NB = 512
LAG = 3
R = 64

F32 = mybir.dt.float32
BF16 = mybir.dt.bfloat16
I32 = mybir.dt.int32
ALU = mybir.AluOpType
ACT = mybir.ActivationFunctionType


def sizes(n_nodes, n_edges):
    chunks = -(-n_edges // CE)
    blocks = 2 * -(-(n_nodes + 1 + 2 * P) // (2 * NB))
    return chunks, blocks * NB


def gnn_kernel(nc, n_nodes, ins, out):
    T = ins["src_col"].shape[1]
    CH = T // CT
    NROWS = ins["x"].shape[0]
    NT = NROWS // P
    BLOCKS = NROWS // NB
    SPARE = NROWS - P
    EPAD = T * P
    HIS = NT
    ZEROS = NROWS // 4

    ctx = ExitStack()
    with ctx:
        def dram(name, shape, dt):
            return nc.dram_tensor(name, shape, dt, kind="Internal").ap()

        y_tab = dram("y_tab", [NROWS, P], F32)
        v_tab = dram("v_tab", [NROWS, P], F32)
        x1_tab = dram("x1_tab", [NROWS, P], F32)
        xT_tab = dram("xT_tab", [P, NROWS], F32)
        uT_tab = dram("uT_tab", [P, NROWS], F32)
        rows_tab = dram("rows_tab", [2, 2, EPAD], BF16)
        conv_acc = [dram(f"conv_acc{q}", [NROWS, P], F32) for q in range(ACCS)]
        pair_acc = [dram(f"pair_acc{q}", [NROWS, P], F32) for q in range(ACCS)]

        stage = [ctx]

        def sb(name, shape, dt=F32):
            return stage[-1].enter_context(nc.sbuf_tensor(name, shape, dt))

        def ps(name, shape, dt=F32):
            return stage[-1].enter_context(nc.psum_tensor(name, shape, dt))

        def sem(name):
            return stage[-1].enter_context(nc.semaphore(name))

        src_i = sb("src_i", [P, T], I32)
        dst_i = sb("dst_i", [P, T], I32)
        src_f = sb("src_f", [P, T])
        dst_f = sb("dst_f", [P, T])
        ident = sb("ident", [P, P])
        not_earlier = sb("not_earlier", [P, P])
        spare_row = sb("spare_row", [P, 1])
        hilo_w = sb("hilo_w", [2, P], BF16)
        ones_row = sb("ones_row", [1, P])
        dis = sb("dis", [P, NT])
        zeros = sb("zeros", [P, ZEROS])

        with ExitStack() as s:
            stage.append(s)
            NG = T // 8
            rows_i = sb("rows_i", [P, 2, T], I32)
            part_i = sb("part_i", [P, 2, T], I32)
            rows_b = sb("rows_b", [P, 2, 2, T], BF16)
            dst_hi = sb("dst_hi", [P, T])
            dst_lo = sb("dst_lo", [P, T])
            iota_i = sb("iota_i", [P, P], I32)
            iota = sb("iota", [P, P])
            row_i = sb("row_i", [P, 1], I32)
            hi_w = sb("hi_w", [2, 1])
            hi_hot = sb("hi_hot", [P, 2, 8, HIS], BF16)
            lo_hot = sb("lo_hot", [P, 2, 8, P], BF16)
            deg_ps = ps("deg_ps", [P, HIS])
            deg = sb("deg", [P, NT])
            degc = sb("degc", [P, NT])
            half = sb("half", [P, NT])
            rsq = sb("rsq", [P, NT])
            cols_in, rows_in, dve_own, iota_made = sem("cols_in"), sem("rows_in"), sem("dve_own"), sem("iota_made")
            rows_made, rows_out, hots, hots_used = sem("rows_made"), sem("rows_out"), sem("hots"), sem("hots_used")
            pool_own, tri_made, clamped, rooted = sem("pool_own"), sem("tri_made"), sem("clamped"), sem("rooted")
            mm_zero, zeros_made, dis_made, cleared = sem("mm_zero"), sem("zeros_made"), sem("dis_made"), sem("cleared")

            with nc.Block() as block:
                @block.sync
                def _(sp):
                    sp.dma_start(dst_i[:, :], ins["dst_col"]).then_inc(cols_in, 16)
                    sp.dma_start(src_i[:, :], ins["src_col"]).then_inc(cols_in, 16)
                    sp.dma_start(rows_i[:, 0, :], ins["src_row"]).then_inc(rows_in, 16)
                    sp.dma_start(rows_i[:, 1, :], ins["dst_row"]).then_inc(rows_in, 16)
                    sp.wait_ge(rows_made, 1)
                    for k in range(2):
                        for s_ in range(2):
                            sp.dma_start(rows_tab[k, s_, :].rearrange("(p t) -> p t", t=T),
                                         rows_b[:, k, s_, :]).then_inc(rows_out, 16)
                    sp.wait_ge(rows_out, 64)

                @block.gpsimd
                def _(pool):
                    pool.iota(iota_i[:, :], [[1, P]], base=0, channel_multiplier=0).then_inc(iota_made, 1)
                    pool.iota(row_i[:, :], [[0, 1]], base=SPARE, channel_multiplier=1).then_inc(iota_made, 1)
                    pool.memset(ident[:, :], 0.0).then_inc(pool_own, 1)
                    pool.memset(not_earlier[:, :], 1.0).then_inc(pool_own, 1)
                    pool.memset(hi_w[:, :], 1.0).then_inc(pool_own, 1)
                    pool.wait_ge(pool_own, 3)
                    pool.affine_select(out=ident[:, :], in_=ident[:, :], compare_op=ALU.not_equal, fill=1.0,
                                       base=0, pattern=[[-1, P]], channel_multiplier=1).then_inc(tri_made, 1)
                    pool.affine_select(out=not_earlier[:, :], in_=not_earlier[:, :], compare_op=ALU.is_ge,
                                       fill=0.0, base=0, pattern=[[-1, P]],
                                       channel_multiplier=1).then_inc(tri_made, 1)
                    pool.affine_select(out=hi_w[:, :], in_=hi_w[:, :], compare_op=ALU.not_equal, fill=128.0,
                                       base=0, pattern=[[0, 1]], channel_multiplier=1).then_inc(tri_made, 1)
                    pool.wait_ge(clamped, 2)
                    pool.tensor_tensor(rsq[:, :], degc[:, :], half[:, :], ALU.pow).then_inc(rooted, 1)

                @block.vector
                def _(dve):
                    dve.memset(zeros[:, :], 0.0)
                    dve.memset(half[:, :], -0.5)
                    dve.memset(ones_row[:, :], 1.0)
                    dve.memset(hilo_w[:, :], 1.0).then_inc(zeros_made, 1)
                    dve.wait_ge(iota_made, 2)
                    dve.tensor_copy(iota[:, :], iota_i[:, :])
                    dve.tensor_copy(spare_row[:, :], row_i[:, :])
                    dve.wait_ge(cols_in, 32)
                    dve.tensor_scalar(part_i[:, 0, :], dst_i[:, :], 7, None, ALU.arith_shift_right)
                    dve.tensor_scalar(part_i[:, 1, :], dst_i[:, :], 127, None, ALU.bitwise_and).then_inc(dve_own, 1)
                    dve.tensor_copy(dst_f[:, :], dst_i[:, :])
                    dve.tensor_copy(src_f[:, :], src_i[:, :])
                    dve.wait_ge(dve_own, 1)
                    dve.tensor_copy(dst_hi[:, :], part_i[:, 0, :])
                    dve.tensor_copy(dst_lo[:, :], part_i[:, 1, :]).then_inc(dve_own, 1)
                    dve.wait_ge(dve_own, 2)

                    def one_hots(par, t):
                        dve.tensor_tensor(lo_hot[:, par, :, :],
                                          iota[:, :].unsqueeze(1).to_broadcast([P, 8, P]),
                                          dst_lo[:, bass.ds(t, 8)].unsqueeze(2).to_broadcast([P, 8, P]), ALU.is_equal)
                        return dve.tensor_tensor(hi_hot[:, par, :, :],
                                                 iota[:, 0:HIS].unsqueeze(1).to_broadcast([P, 8, HIS]),
                                                 dst_hi[:, bass.ds(t, 8)].unsqueeze(2).to_broadcast([P, 8, HIS]),
                                                 ALU.is_equal)

                    with dve.Fori(0, NG // 2) as i:
                        for par in range(2):
                            dve.wait_ge(hots_used, 2 * i + par + 1)
                            one_hots(par, (2 * i + par) * 8).then_inc(hots, 1)
                    if NG % 2:
                        dve.wait_ge(hots_used, NG)
                        one_hots(0, (NG - 1) * 8).then_inc(hots, 1)

                    dve.wait_ge(rows_in, 32)
                    dve.tensor_scalar(part_i[:, :, :], rows_i[:, :, :], 7, None, ALU.arith_shift_right).then_inc(dve_own, 1)
                    dve.wait_ge(dve_own, 3)
                    dve.tensor_copy(rows_b[:, 0, :, :], part_i[:, :, :]).then_inc(dve_own, 1)
                    dve.wait_ge(dve_own, 4)
                    dve.tensor_scalar(part_i[:, :, :], rows_i[:, :, :], 127, None, ALU.bitwise_and).then_inc(dve_own, 1)
                    dve.wait_ge(dve_own, 5)
                    dve.tensor_copy(rows_b[:, 1, :, :], part_i[:, :, :]).then_inc(rows_made, 1)
                    dve.wait_ge(tri_made, 3)
                    dve.tensor_scalar(hilo_w[:, :], hilo_w[:, :], hi_w[:, 0:1], None, ALU.mult)

                    dve.wait_ge(hots_used, NG + 3)
                    dve.tensor_copy(deg[:, :], deg_ps[:, 0:NT]).then_inc(dve_own, 1)
                    dve.wait_ge(dve_own, 6)
                    dve.tensor_scalar(degc[:, :], deg[:, :], 1.0, None, ALU.max).then_inc(clamped, 2)
                    dve.wait_ge(rooted, 1)
                    dve.scalar_tensor_tensor(out=dis[:, :], in0=deg[:, :], scalar=0.0, in1=rsq[:, :],
                                             op0=ALU.is_gt, op1=ALU.mult).then_inc(dis_made, 1)

                @block.tensor
                def _(pe):
                    pe.sem_inc(hots_used, 2)
                    pe.wait_ge(zeros_made, 1)
                    zb = zeros[:, 0:P]
                    pe.matmul(deg_ps[:, :], zb, zeros[:, 0:HIS], start=True, stop=False)

                    def count(par):
                        for k in range(8):
                            m = pe.matmul(deg_ps[:, :], lo_hot[:, par, k, :], hi_hot[:, par, k, :],
                                          start=False, stop=False)
                        m.then_inc(hots_used, 1)

                    with pe.Fori(0, NG // 2) as i:
                        for par in range(2):
                            pe.wait_ge(hots, 2 * i + par + 1)
                            count(par)
                    if NG % 2:
                        pe.wait_ge(hots, NG)
                        count(0)
                    pe.matmul(deg_ps[:, :], zb, zeros[:, 0:HIS], start=False, stop=True).then_inc(hots_used, 1)
            stage.pop()

        with ExitStack() as s:
            stage.append(s)
            xs = sb("xs", [P, NT, P])
            x_in, y_made, y_out = sem("x_in"), sem("y_made"), sem("y_out")
            with nc.Block() as block:
                @block.sync
                def _(sp):
                    sp.dma_start(xs[:, :, :], ins["x"].rearrange("(t p) f -> p t f", p=P)).then_inc(x_in, 16)
                    sp.wait_ge(y_made, 1)
                    sp.dma_start(y_tab.rearrange("(t p) f -> p t f", p=P), xs[:, :, :]).then_inc(y_out, 16)
                    sp.wait_ge(y_out, 16)

                @block.vector
                def _(dve):
                    dve.wait_ge(x_in, 16)
                    dve.tensor_tensor(xs[:, :, :], xs[:, :, :], dis[:, :].unsqueeze(2).to_broadcast([P, NT, P]),
                                      ALU.mult).then_inc(y_made, 1)
            stage.pop()

        def scatter_pass(tag, table, gather_i, target, target_f, acc, edge_product):
            with ExitStack() as s:
                stage.append(s)

                def named(name):
                    return sem(f"{tag}_{name}")

                wg = sb(tag + "wg", [R, P])
                rows = sb(tag + "rows", [2, CG, GE], BF16)
                attr = sb(tag + "attr", [R, CG, GE])
                gidx = sb(tag + "gidx", [P, CG, GT], I32)
                got = sb(tag + "got", [P, CG, GE])
                tcol = sb(tag + "tcol", [P, CT])
                same = sb(tag + "same", [P, 2, GE])
                prod = sb(tag + "prod", [P, 2, GE])
                earlier = sb(tag + "earlier", [P, 2, GT])
                shifted = sb(tag + "shifted", [P, CT])
                pick = sb(tag + "pick", [P, 2, GT])
                sidx = sb(tag + "sidx", [P, CG, GT], I32)
                summed = sb(tag + "summed", [P, CG, GE])
                rows_ps = ps(tag + "rows_ps", [P, 2, GE])
                filt_ps = ps(tag + "filt_ps", [P, 2, GE])
                sum_ps = ps(tag + "sum_ps", [P, 2, GE])

                w_in = named("w_in")
                rows_in = [named(f"rows_in{g}") for g in range(CG)]
                attr_in = [named(f"attr_in{g}") for g in range(CG)]
                got_in = [named(f"got_in{g}") for g in range(CG)]
                acc_done = [named(f"acc_done{q}") for q in range(ACCS)]
                rows_made = named("rows_made")
                same_made = named("same_made")
                counted = named("counted")
                columns = named("columns")
                filt_made = named("filt_made")
                prod_made = named("prod_made")
                sums_made = named("sums_made")
                sums_out = named("sums_out")
                sidx_made = named("sidx_made")
                gidx_made = named("gidx_made")
                pool_passed = named("pool_passed")
                sync_passed = named("sync_passed")

                def done(n):
                    return n + (CG + 1)

                with nc.Block() as block:
                    @block.sync
                    def _(sp):
                        sp.dma_start(wg[:, :], ins["WgT"]).then_inc(w_in, 16)
                        with sp.Fori(0, CH) as c:
                            for g in range(CG):
                                sp.wait_ge(rows_made, done(c * CG + g - CG))
                                sp.sem_inc(sync_passed, 1)
                                sp.dma_start(rows[:, g, :], rows_tab[:, target, bass.ds(c * CE + g * GE, GE)]
                                             ).then_inc(rows_in[g], 16)
                                if edge_product:
                                    sp.wait_ge(filt_made, done(c * CG + g - CG))
                                    sp.sem_inc(sync_passed, 1)
                                    sp.dma_start(attr[:, g, :],
                                                 ins["attr_t"][:, bass.ds(c * CE + g * GE, GE)]
                                                 ).then_inc(attr_in[g], 16)

                    @block.gpsimd
                    def _(pool):
                        for q in range(ACCS):
                            pool.dma_start(acc[q].rearrange("(p a) f -> p (a f)", p=P),
                                           zeros[:, :].unsqueeze(1).to_broadcast([P, NROWS // ZEROS, ZEROS])
                                           ).then_inc(acc_done[q], 16)

                        def gather(c, g):
                            n = c * CG + g
                            pool.wait_ge(gidx_made, done(n))
                            pool.wait_ge(prod_made if edge_product else sums_made, done(n - CG))
                            pool.sem_inc(pool_passed, 1)
                            for k in range(GT):
                                pool.indirect_dma_start(
                                    out=got[:, g, k * P:(k + 1) * P], out_offset=None, in_=table,
                                    in_offset=bass.IndirectOffsetOnAxis(ap=gidx[:, g, k:k + 1], axis=0)
                                ).then_inc(got_in[g], 16)

                        def scatter(c, g):
                            n = c * CG + g
                            pool.wait_ge(sums_out, done(n))
                            pool.wait_ge(sidx_made, done(n))
                            for k in range(GT):
                                t = g * GT + k
                                q = t % ACCS
                                pool.wait_ge(acc_done[q], c * (CT // ACCS * 16) + (1 + t // ACCS) * 16)
                                pool.sem_inc(pool_passed, 1)
                                pool.indirect_dma_start(
                                    out=acc[q], out_offset=bass.IndirectOffsetOnAxis(ap=sidx[:, g, k:k + 1], axis=0),
                                    in_=summed[:, g, k * P:(k + 1) * P], in_offset=None, compute_op=ALU.add
                                ).then_inc(acc_done[q], 16)

                        def chunk(c, last):
                            for g in range(CG):
                                if g + LAG < CG:
                                    gather(c, g + LAG)
                                elif not last:
                                    gather(c + 1, g + LAG - CG)
                                scatter(c, g)

                        for g in range(LAG):
                            gather(0, g)
                        with pool.Fori(0, CH - 1) as c:
                            chunk(c, False)
                        chunk(CH - 1, True)
                        for q in range(ACCS):
                            pool.wait_ge(acc_done[q], (CH * (CT // ACCS) + 1) * 16)

                    @block.tensor
                    def _(pe):
                        pe.sem_inc(rows_made, CG)
                        pe.sem_inc(filt_made, CG)
                        pe.sem_inc(sums_made, CG)
                        pe.wait_ge(w_in, 16)

                        def front(c, g):
                            n = c * CG + g
                            h = g % 2
                            pe.wait_ge(rows_in[g], c * 16 + 16)
                            pe.wait_ge(same_made, done(n - 2))
                            pe.matmul(rows_ps[:, h, :], hilo_w[:, :], rows[:, g, :], start=True, stop=True
                                      ).then_inc(rows_made, 1)
                            if edge_product:
                                pe.wait_ge(attr_in[g], c * 16 + 16)
                                pe.wait_ge(prod_made, done(n - 2))
                                for k in range(GT):
                                    col = slice(k * P, (k + 1) * P)
                                    m = pe.matmul(filt_ps[:, h, col], attr[:, g, col], wg[:, :], start=True, stop=True)
                                m.then_inc(filt_made, 1)

                        def back(c, g):
                            n = c * CG + g
                            h = g % 2
                            pe.wait_ge(same_made, done(n))
                            pe.wait_ge(sums_out, done(n - 2))
                            if edge_product:
                                pe.wait_ge(prod_made, done(n))
                                values = prod[:, h, :]
                            else:
                                pe.wait_ge(got_in[g], c * (GT * 16) + GT * 16)
                                values = got[:, g, :]
                            for k in range(GT):
                                col = slice(k * P, (k + 1) * P)
                                m = pe.matmul(sum_ps[:, h, col], same[:, h, col], values[:, col], start=True, stop=True)
                            m.then_inc(sums_made, 1)

                        def chunk(c, last):
                            for g in range(CG):
                                if g + 1 < CG:
                                    front(c, g + 1)
                                elif not last:
                                    front(c + 1, 0)
                                back(c, g)

                        front(0, 0)
                        with pe.Fori(0, CH - 1) as c:
                            chunk(c, False)
                        chunk(CH - 1, True)

                    @block.vector
                    def _(dve):
                        dve.sem_inc(same_made, CG)
                        dve.sem_inc(prod_made, CG)
                        dve.sem_inc(gidx_made, CG)
                        for g in range(CG):
                            dve.tensor_copy(gidx[:, g, :], gather_i[:, g * GT:(g + 1) * GT]).then_inc(gidx_made, 1)

                        def chunk(c, last):
                            dve.tensor_copy(tcol[:, :], target_f[:, bass.ds(c * CT, CT)]).then_inc(columns, 1)
                            dve.wait_ge(columns, c * 2 + 1)
                            dve.tensor_scalar(shifted[:, :], tcol[:, :], spare_row[:, 0:1], None,
                                              ALU.subtract).then_inc(columns, 1)
                            dve.wait_ge(columns, c * 2 + 2)
                            for g in range(CG):
                                n = c * CG + g
                                h = g % 2
                                dve.wait_ge(rows_made, done(n))
                                dve.wait_ge(sums_made, done(n - 2))
                                for k in range(GT):
                                    col = slice(k * P, (k + 1) * P)
                                    t = g * GT + k
                                    m = dve.scalar_tensor_tensor(
                                        out=same[:, h, col], in0=rows_ps[:, h, col], scalar=tcol[:, t:t + 1],
                                        in1=not_earlier[:, :], op0=ALU.is_equal, op1=ALU.mult,
                                        accum_out=earlier[:, h, k:k + 1])
                                m.then_inc(counted, 1)
                                dve.wait_ge(counted, n + 1)
                                dve.wait_ge(sidx_made, done(n - 2))
                                dve.scalar_tensor_tensor(
                                    out=pick[:, h, :], in0=earlier[:, h, :], scalar=1.5,
                                    in1=shifted[:, g * GT:(g + 1) * GT], op0=ALU.is_lt, op1=ALU.mult
                                ).then_inc(same_made, 1)
                                if edge_product or not last:
                                    dve.wait_ge(got_in[g], c * (GT * 16) + GT * 16)
                                if edge_product:
                                    dve.wait_ge(filt_made, done(n))
                                    dve.tensor_tensor(prod[:, h, :], filt_ps[:, h, :], got[:, g, :],
                                                      ALU.mult).then_inc(prod_made, 1)
                                if not last:
                                    dve.tensor_copy(gidx[:, g, :], gather_i[:, bass.ds(c * CT + (CT + g * GT), GT)]
                                                    ).then_inc(gidx_made, 1)

                        with dve.Fori(0, CH - 1) as c:
                            chunk(c, False)
                        chunk(CH - 1, True)

                    @block.scalar
                    def _(act):
                        act.sem_inc(sums_out, CG)
                        act.sem_inc(sidx_made, CG)
                        with act.Fori(0, CH) as c:
                            for g in range(CG):
                                n = c * CG + g
                                h = g % 2
                                for k in range(GT):
                                    t = g * GT + k
                                    act.wait_ge(acc_done[t % ACCS],
                                                c * (CT // ACCS * 16) + (1 + t // ACCS) * 16)
                                act.wait_ge(same_made, done(n))
                                act.activation(sidx[:, g, :], pick[:, h, :], ACT.Identity,
                                               bias=spare_row[:, 0:1]).then_inc(sidx_made, 1)
                                act.wait_ge(sums_made, done(n))
                                act.copy(summed[:, g, :], sum_ps[:, h, :]).then_inc(sums_out, 1)
                stage.pop()

        scatter_pass("conv", y_tab, src_i, 1, dst_f, conv_acc, False)

        WI, WJ, W1, W2, WV = 0, 1, 2, 5, 8
        BI, B1, B2, BV, GATE = 0, 1, 4, 7, 8
        CAP = 40.0
        EPS = 1e-5
        PAIRS = BLOCKS // 2

        with ExitStack() as s:
            stage.append(s)
            wts = sb("n1wts", [P, 2, P])
            bi_col = sb("n1bi", [P, 9])
            bj_row = sb("n1bj", [1, P])
            parts = sb("n1parts", [P, 2, ACCS, NB])
            xin = sb("n1xin", [P, 2, NB])
            hid = sb("n1hid", [P, 2, NB])
            x1 = sb("n1x1", [P, 2, NB])
            xp = sb("n1xp", [P, 2, NB])
            xT = sb("n1xT", [P, 2, NB])
            low = sb("n1low", [P, 2, 2, NB])
            ex = sb("n1ex", [P, 2, 2, NB])
            vu = sb("n1vu", [P, 2, 2, NB])
            stats = sb("n1stats", [P, 2, 4, 6])
            mv = sb("n1mv", [P, 2, 4, 2])
            var = sb("n1var", [P, 2, 4])
            rstd = sb("n1rstd", [P, 2, 4])
            half4 = sb("n1half", [P, 4])
            one_ps = [ps(f"n1one{h}", [P, NB]) for h in range(2)]
            two_ps = [ps(f"n1two{h}", [P, NB]) for h in range(2)]
            names = ("summed", "scaled", "joined", "stats", "mv", "var", "rstd", "x1", "low", "ex", "ln", "xp",
                     "xTps", "xT", "vups", "low2", "ex2", "ln2", "vu", "stored")
            sm = {k: sem("n1_" + k) for k in names}
            w_in = sem("n1_w_in")
            sync_passed = sem("n1_sync_passed")
            half_made = sem("n1_half_made")
            loaded = [sem(f"n1_loaded{h}") for h in range(2)]
            stores = [sem(f"n1_stores{h}") for h in range(2)]

            def done(n):
                return n + 3

            with nc.Block() as block:
                @block.sync
                def _(sp):
                    sp.dma_start(wts[:, :, :], ins["WT"][:, WI:WI + 2, :]).then_inc(w_in, 16)
                    sp.dma_start(bi_col[:, :], ins["cols"]).then_inc(w_in, 16)
                    sp.dma_start(bj_row[:, :], ins["bj"]).then_inc(w_in, 16)

                    def load(i, h):
                        at = bass.ds(i * (2 * NB) + h * NB, NB)
                        for q in range(ACCS):
                            sp.dma_start(parts[:, h, q, :].rearrange("p (j f) -> p j f", f=P),
                                         conv_acc[q][at, :].rearrange("(j p) f -> p j f", p=P)).then_inc(loaded[h], 16)
                        sp.dma_start(xin[:, h, :].rearrange("p (j f) -> p j f", f=P),
                                     ins["x"][at, :].rearrange("(j p) f -> p j f", p=P)).then_inc(loaded[h], 16)

                    def pair(i, last):
                        for h in range(2):
                            if not last:
                                sp.wait_ge(sm["joined"], i * 2 + h + 1)
                                sp.sem_inc(sync_passed, 1)
                                load(i + 1, h)
                        for h in range(2):
                            at = bass.ds(i * (2 * NB) + h * NB, NB)
                            sp.wait_ge(sm["x1"], i * 2 + h + 1)
                            sp.sem_inc(sync_passed, 1)
                            sp.dma_start(x1_tab[at, :].rearrange("(j p) f -> p j f", p=P),
                                         x1[:, h, :].rearrange("p (j f) -> p j f", f=P)).then_inc(stores[h], 16)
                        for h in range(2):
                            at = bass.ds(i * (2 * NB) + h * NB, NB)
                            sp.wait_ge(sm["xT"], i * 2 + h + 1)
                            sp.sem_inc(sync_passed, 1)
                            sp.dma_start(xT_tab[:, at], xT[:, h, :]).then_inc(stores[h], 16)
                        for h in range(2):
                            at = bass.ds(i * (2 * NB) + h * NB, NB)
                            sp.wait_ge(sm["vu"], done(i * 2 + h))
                            sp.sem_inc(sync_passed, 1)
                            sp.dma_start(v_tab[at, :].rearrange("(j p) f -> p j f", p=P),
                                         vu[:, h, 0, :].rearrange("p (j f) -> p j f", f=P)).then_inc(stores[h], 16)
                            sp.dma_start(uT_tab[:, at], vu[:, h, 1, :]).then_inc(stores[h], 16)
                        for h in range(2):
                            sp.wait_ge(stores[h], i * 64 + 64)
                            sp.sem_inc(sm["stored"], 1)

                    sp.sem_inc(sm["stored"], 2)
                    load(0, 0)
                    load(0, 1)
                    if PAIRS > 1:
                        with sp.Fori(0, PAIRS - 1) as i:
                            pair(i, False)
                    pair(PAIRS - 1, True)

                @block.gpsimd
                def _(pool):
                    pool.memset(half4[:, :], -0.5).then_inc(half_made, 1)
                    pool.wait_ge(half_made, 1)
                    with pool.Fori(0, PAIRS) as i:
                        for h in range(2):
                            pool.wait_ge(sm["var"], i * 2 + h + 1)
                            pool.tensor_tensor(rstd[:, h, :], var[:, h, :], half4[:, :], ALU.pow).then_inc(sm["rstd"], 1)

                @block.vector
                def _(dve):
                    dve.sem_inc(sm["vu"], 2)
                    dve.wait_ge(w_in, 48)
                    with dve.Fori(0, PAIRS) as i:
                        for h in range(2):
                            dve.wait_ge(sm["summed"], i * 2 + h + 1)
                            d = dis[:, bass.ds(i * 8 + h * 4, 4)].unsqueeze(2).to_broadcast([P, 4, P])
                            dve.tensor_tensor(hid[:, h, :].rearrange("p (j f) -> p j f", f=P),
                                              one_ps[h][:, :].rearrange("p (j f) -> p j f", f=P), d,
                                              ALU.mult).then_inc(sm["scaled"], 1)
                        for h in range(2):
                            dve.wait_ge(sm["scaled"], i * 2 + h + 1)
                            dve.wait_ge(loaded[h], i * (16 * (ACCS + 1)) + 16 * (ACCS + 1))
                            dve.scalar_tensor_tensor(out=hid[:, h, :], in0=hid[:, h, :], scalar=0.0, in1=xin[:, h, :],
                                                     op0=ALU.max, op1=ALU.add).then_inc(sm["joined"], 1)
                        for h in range(2):
                            dve.wait_ge(sm["joined"], i * 2 + h + 1)
                            for j in range(4):
                                m = dve.bn_stats(stats[:, h, j, :], hid[:, h, j * P:(j + 1) * P])
                            m.then_inc(sm["stats"], 1)
                        for h in range(2):
                            dve.wait_ge(sm["stats"], 1)
                            dve.wait_ge(sm["stats"], i * 2 + h + 1)
                            for j in range(4):
                                m = dve.bn_aggr(mv[:, h, j, :], stats[:, h, j, :])
                            m.then_inc(sm["mv"], 1)
                        for h in range(2):
                            dve.wait_ge(sm["mv"], i * 2 + h + 1)
                            dve.tensor_scalar(var[:, h, :], mv[:, h, :, 1], EPS, None, ALU.add).then_inc(sm["var"], 1)
                        for h in range(2):
                            dve.wait_ge(sm["rstd"], i * 2 + h + 1)
                            dve.wait_ge(sm["stored"], done(i * 2 + h - 2))
                            for j in range(4):
                                col = slice(j * P, (j + 1) * P)
                                m = dve.tensor_scalar(x1[:, h, col], hid[:, h, col], mv[:, h, j, 0:1],
                                                      rstd[:, h, j:j + 1], ALU.subtract, ALU.mult)
                            m.then_inc(sm["x1"], 1)
                        for h in range(2):
                            dve.wait_ge(sm["x1"], i * 2 + h + 1)
                            dve.tensor_scalar(low[:, h, 0, :], x1[:, h, :], CAP, None, ALU.min).then_inc(sm["low"], 1)
                        for h in range(2):
                            dve.wait_ge(sm["ln"], i * 2 + h + 1)
                            dve.tensor_tensor(xp[:, h, :], x1[:, h, :], low[:, h, 0, :], ALU.max).then_inc(sm["xp"], 1)
                        for h in range(2):
                            dve.wait_ge(sm["vups"], i * 2 + h + 1)
                            dve.tensor_scalar(low[:, h, 0, :], two_ps[h][:, :], CAP, None, ALU.min)
                            dve.tensor_scalar(low[:, h, 1, :], one_ps[h][:, :], bi_col[:, BI:BI + 1], CAP, ALU.add,
                                              ALU.min).then_inc(sm["low2"], 1)
                        for h in range(2):
                            dve.wait_ge(sm["ln2"], i * 2 + h + 1)
                            dve.tensor_tensor(vu[:, h, 0, :], two_ps[h][:, :], low[:, h, 0, :], ALU.max)
                            dve.scalar_tensor_tensor(out=vu[:, h, 1, :], in0=one_ps[h][:, :], scalar=bi_col[:, BI:BI + 1],
                                                     in1=low[:, h, 1, :], op0=ALU.add, op1=ALU.max
                                                     ).then_inc(sm["vu"], 1)

                @block.scalar
                def _(act):
                    with act.Fori(0, PAIRS) as i:
                        for h in range(2):
                            act.wait_ge(sm["low"], i * 2 + h + 1)
                            act.activation(ex[:, h, 0, :], low[:, h, 0, :], ACT.Exp).then_inc(sm["ex"], 1)
                        for h in range(2):
                            act.wait_ge(sm["ex"], i * 2 + h + 1)
                            act.activation(low[:, h, 0, :], ex[:, h, 0, :], ACT.Ln, bias=1.0).then_inc(sm["ln"], 1)
                        for h in range(2):
                            act.wait_ge(sm["xTps"], i * 2 + h + 1)
                            act.wait_ge(sm["stored"], done(i * 2 + h - 2))
                            act.copy(xT[:, h, :], one_ps[h][:, :]).then_inc(sm["xT"], 1)
                        for h in range(2):
                            act.wait_ge(sm["low2"], i * 2 + h + 1)
                            act.activation(ex[:, h, :, :], low[:, h, :, :], ACT.Exp).then_inc(sm["ex2"], 1)
                        for h in range(2):
                            act.wait_ge(sm["ex2"], i * 2 + h + 1)
                            act.activation(low[:, h, :, :], ex[:, h, :, :], ACT.Ln, bias=1.0).then_inc(sm["ln2"], 1)

                @block.tensor
                def _(pe):
                    pe.wait_ge(w_in, 48)
                    with pe.Fori(0, PAIRS) as i:
                        for h in range(2):
                            pe.wait_ge(loaded[h], i * (16 * (ACCS + 1)) + 16 * (ACCS + 1))
                            pe.wait_ge(sm["vu"], done(i * 2 + h - 2))
                            for q in range(ACCS):
                                m = pe.matmul(one_ps[h][:, :], ident[:, :], parts[:, h, q, :], start=q == 0,
                                              stop=q == ACCS - 1)
                            m.then_inc(sm["summed"], 1)
                        for h in range(2):
                            pe.wait_ge(sm["xp"], i * 2 + h + 1)
                            for j in range(4):
                                col = slice(j * P, (j + 1) * P)
                                m = pe.transpose(one_ps[h][:, col], xp[:, h, col], ident[:, :])
                            m.then_inc(sm["xTps"], 1)
                        for h in range(2):
                            pe.wait_ge(sm["xT"], i * 2 + h + 1)
                            for j in range(4):
                                col = slice(j * P, (j + 1) * P)
                                pe.matmul(two_ps[h][:, col], ones_row[:, :], bj_row[:, :], start=True, stop=False)
                                pe.matmul(two_ps[h][:, col], xT[:, h, col], wts[:, WJ, :], start=False, stop=True)
                            pe.matmul(one_ps[h][:, :], wts[:, WI, :], xT[:, h, :], start=True, stop=True
                                      ).then_inc(sm["vups"], 1)
            stage.pop()

        scatter_pass("pair", v_tab, dst_i, 0, src_f, pair_acc, True)

        with ExitStack() as s:
            stage.append(s)
            wts = sb("n2wts", [P, 9, P])
            cols = sb("n2cols", [P, 9])
            parts = sb("n2parts", [P, 2, ACCS, NB])
            x1 = sb("n2x1", [P, 2, NB])
            xT = sb("n2xT", [P, 2, NB])
            u0 = sb("n2u0", [P, 2, NB])
            u = sb("n2u", [P, 2, NB])
            low = sb("n2low", [P, 2, NB])
            ex = sb("n2ex", [P, 2, NB])
            sp_u = sb("n2sp", [P, 2, NB])
            gx = sb("n2gx", [P, 2, NB])
            res = sb("n2res", [P, 2, NB])
            stats = sb("n2stats", [P, 2, 4, 6])
            mv = sb("n2mv", [P, 2, 4, 2])
            var = sb("n2var", [P, 2, 4])
            rstd = sb("n2rstd", [P, 2, 4])
            half4 = sb("n2half", [P, 4])
            one_ps = [ps(f"n2one{h}", [P, NB]) for h in range(2)]
            two_ps = [ps(f"n2two{h}", [P, NB]) for h in range(2)]
            names = ("summed", "low", "ex", "ln", "sp", "mm", "u", "gx", "o", "oT", "joined", "stats", "mv", "var",
                     "rstd", "res", "stored")
            sm2 = {k: sem("n2_" + k) for k in names}
            w_in = sem("n2_w_in")
            sync_passed = sem("n2_sync_passed")
            half_made = sem("n2_half_made")
            loaded = [sem(f"n2_loaded{h}") for h in range(2)]
            stores = [sem(f"n2_stores{h}") for h in range(2)]
            LOADS = (ACCS + 3) * 16
            SOFTS = 7
            MMS = 7

            def done(n):
                return n + 3

            def nth(i, many, k, h):
                return i * (2 * many) + (2 * k + h + 1)

            with nc.Block() as block:
                @block.sync
                def _(sp):
                    sp.dma_start(wts[:, :, :], ins["WT"]).then_inc(w_in, 16)
                    sp.dma_start(cols[:, :], ins["cols"]).then_inc(w_in, 16)

                    def load(i, h):
                        at = bass.ds(i * (2 * NB) + h * NB, NB)
                        for q in range(ACCS):
                            sp.dma_start(parts[:, h, q, :].rearrange("p (j f) -> p j f", f=P),
                                         pair_acc[q][at, :].rearrange("(j p) f -> p j f", p=P)).then_inc(loaded[h], 16)
                        sp.dma_start(x1[:, h, :].rearrange("p (j f) -> p j f", f=P),
                                     x1_tab[at, :].rearrange("(j p) f -> p j f", p=P)).then_inc(loaded[h], 16)
                        sp.dma_start(xT[:, h, :], xT_tab[:, at]).then_inc(loaded[h], 16)
                        sp.dma_start(u0[:, h, :], uT_tab[:, at]).then_inc(loaded[h], 16)

                    def pair(i, last):
                        for h in range(2):
                            at = bass.ds(i * (2 * NB) + h * NB, NB)
                            sp.wait_ge(sm2["joined"], i * 2 + h + 1)
                            sp.sem_inc(sync_passed, 1)
                            if not last:
                                load(i + 1, h)
                            sp.wait_ge(sm2["res"], done(i * 2 + h))
                            sp.sem_inc(sync_passed, 1)
                            sp.dma_start(out[at, :].rearrange("(j p) f -> p j f", p=P),
                                         res[:, h, :].rearrange("p (j f) -> p j f", f=P)).then_inc(stores[h], 16)
                        for h in range(2):
                            sp.wait_ge(stores[h], i * 16 + 16)
                            sp.sem_inc(sm2["stored"], 1)

                    sp.sem_inc(sm2["stored"], 2)
                    load(0, 0)
                    load(0, 1)
                    if PAIRS > 1:
                        with sp.Fori(0, PAIRS - 1) as i:
                            pair(i, False)
                    pair(PAIRS - 1, True)

                @block.gpsimd
                def _(pool):
                    pool.memset(half4[:, :], -0.5).then_inc(half_made, 1)
                    pool.wait_ge(half_made, 1)
                    with pool.Fori(0, PAIRS) as i:
                        for h in range(2):
                            pool.wait_ge(sm2["var"], i * 2 + h + 1)
                            pool.tensor_tensor(rstd[:, h, :], var[:, h, :], half4[:, :], ALU.pow).then_inc(sm2["rstd"], 1)

                @block.vector
                def _(dve):
                    dve.wait_ge(w_in, 32)
                    dve.sem_inc(sm2["res"], 2)
                    with dve.Fori(0, PAIRS) as i:
                        for h in range(2):
                            dve.wait_ge(loaded[h], i * LOADS + LOADS)
                            dve.wait_ge(sm2["summed"], i * 2 + h + 1)
                            dve.wait_ge(sm2["res"], done(i * 2 + h - 2))
                            dve.tensor_tensor(u[:, h, :], u0[:, h, :], one_ps[h][:, :], ALU.add
                                              ).then_inc(sm2["u"], 1)
                            dve.tensor_scalar(gx[:, h, :], xT[:, h, :], cols[:, GATE:GATE + 1], cols[:, BV:BV + 1],
                                              ALU.mult, ALU.add).then_inc(sm2["gx"], 1)
                        for k in range(SOFTS):
                            layer = k // 2
                            inner = k % 2 == 1
                            bias = cols[:, B1 + layer:B1 + layer + 1] if inner else None
                            for h in range(2):
                                if inner:
                                    dve.wait_ge(sm2["mm"], nth(i, MMS, 2 * layer, h))
                                    dve.tensor_scalar(low[:, h, :], one_ps[h][:, :], bias, CAP, ALU.add, ALU.min
                                                      ).then_inc(sm2["low"], 1)
                                else:
                                    dve.wait_ge(sm2["u"], nth(i, 4, layer, h))
                                    dve.tensor_scalar(low[:, h, :], u[:, h, :], CAP, None, ALU.min
                                                      ).then_inc(sm2["low"], 1)
                            for h in range(2):
                                dve.wait_ge(sm2["ln"], nth(i, SOFTS, k, h))
                                if inner:
                                    dve.scalar_tensor_tensor(out=sp_u[:, h, :], in0=one_ps[h][:, :], scalar=bias,
                                                             in1=low[:, h, :], op0=ALU.add, op1=ALU.max
                                                             ).then_inc(sm2["sp"], 1)
                                else:
                                    dve.tensor_tensor(sp_u[:, h, :], u[:, h, :], low[:, h, :], ALU.max
                                                      ).then_inc(sm2["sp"], 1)
                            if inner:
                                for h in range(2):
                                    dve.wait_ge(sm2["mm"], nth(i, MMS, 2 * layer + 1, h))
                                    dve.scalar_tensor_tensor(out=u[:, h, :], in0=two_ps[h][:, :],
                                                             scalar=cols[:, B2 + layer:B2 + layer + 1],
                                                             in1=u[:, h, :], op0=ALU.add, op1=ALU.add
                                                             ).then_inc(sm2["u"], 1)
                        for h in range(2):
                            dve.wait_ge(sm2["mm"], nth(i, MMS, 6, h))
                            dve.wait_ge(sm2["gx"], i * 2 + h + 1)
                            dve.tensor_tensor(gx[:, h, :], one_ps[h][:, :], gx[:, h, :], ALU.add).then_inc(sm2["o"], 1)
                        for h in range(2):
                            dve.wait_ge(sm2["oT"], i * 2 + h + 1)
                            dve.tensor_tensor(u[:, h, :], two_ps[h][:, :], x1[:, h, :], ALU.add
                                              ).then_inc(sm2["joined"], 1)
                        for h in range(2):
                            dve.wait_ge(sm2["joined"], i * 2 + h + 1)
                            for j in range(4):
                                m = dve.bn_stats(stats[:, h, j, :], u[:, h, j * P:(j + 1) * P])
                            m.then_inc(sm2["stats"], 1)
                        for h in range(2):
                            dve.wait_ge(sm2["stats"], 1)
                            dve.wait_ge(sm2["stats"], i * 2 + h + 1)
                            for j in range(4):
                                m = dve.bn_aggr(mv[:, h, j, :], stats[:, h, j, :])
                            m.then_inc(sm2["mv"], 1)
                        for h in range(2):
                            dve.wait_ge(sm2["mv"], i * 2 + h + 1)
                            dve.tensor_scalar(var[:, h, :], mv[:, h, :, 1], EPS, None, ALU.add).then_inc(sm2["var"], 1)
                        for h in range(2):
                            dve.wait_ge(sm2["rstd"], i * 2 + h + 1)
                            dve.wait_ge(sm2["stored"], done(i * 2 + h - 2))
                            for j in range(4):
                                col = slice(j * P, (j + 1) * P)
                                m = dve.tensor_scalar(res[:, h, col], u[:, h, col], mv[:, h, j, 0:1],
                                                      rstd[:, h, j:j + 1], ALU.subtract, ALU.mult)
                            m.then_inc(sm2["res"], 1)

                @block.scalar
                def _(act):
                    with act.Fori(0, PAIRS) as i:
                        for k in range(SOFTS):
                            for h in range(2):
                                act.wait_ge(sm2["low"], nth(i, SOFTS, k, h))
                                act.activation(ex[:, h, :], low[:, h, :], ACT.Exp).then_inc(sm2["ex"], 1)
                            for h in range(2):
                                act.wait_ge(sm2["ex"], nth(i, SOFTS, k, h))
                                act.activation(low[:, h, :], ex[:, h, :], ACT.Ln, bias=1.0).then_inc(sm2["ln"], 1)

                @block.tensor
                def _(pe):
                    pe.wait_ge(w_in, 32)
                    pe.sem_inc(sm2["o"], 2)
                    with pe.Fori(0, PAIRS) as i:
                        for h in range(2):
                            pe.wait_ge(loaded[h], i * LOADS + LOADS)
                            pe.wait_ge(sm2["o"], done(i * 2 + h - 2))
                            for j in range(4):
                                col = slice(j * P, (j + 1) * P)
                                for q in range(ACCS):
                                    m = pe.matmul(one_ps[h][:, col], parts[:, h, q, col], ident[:, :], start=q == 0,
                                                  stop=q == ACCS - 1)
                            m.then_inc(sm2["summed"], 1)
                        for k in range(SOFTS):
                            layer = k // 2
                            w = WV if k == 6 else (W2 if k % 2 else W1) + layer
                            to = two_ps if k % 2 else one_ps
                            for h in range(2):
                                pe.wait_ge(sm2["sp"], nth(i, SOFTS, k, h))
                                pe.matmul(to[h][:, :], wts[:, w, :], sp_u[:, h, :], start=True, stop=True
                                          ).then_inc(sm2["mm"], 1)
                        for h in range(2):
                            pe.wait_ge(sm2["o"], done(i * 2 + h))
                            for j in range(4):
                                col = slice(j * P, (j + 1) * P)
                                m = pe.transpose(two_ps[h][:, col], gx[:, h, col], ident[:, :])
                            m.then_inc(sm2["oT"], 1)
            stage.pop()


def kernel(x, src, dst, edge_attr_64, edge_weight, L1_gnn_Wg, L1_gnn_Wi, L1_gnn_bi, L1_gnn_Wj, L1_gnn_bj,
           L1_gnn_Wv, L1_gnn_bv, L1_gnn_gate, L1_gnn_res_W1, L1_gnn_res_b1, L1_gnn_res_W2, L1_gnn_res_b2):
    import numpy as np
    import concourse.bacc as bacc
    from concourse.bass_utils import run_bass_kernel_spmd

    n, edges = x.shape[0], src.shape[0]
    chunks, nrows = sizes(n, edges)
    tiles = chunks * CT
    epad = tiles * P - edges

    src = np.concatenate([np.asarray(src), np.full(epad, n, src.dtype)])
    dst = np.concatenate([np.asarray(dst), np.full(epad, n, dst.dtype)])
    attr = np.concatenate([np.asarray(edge_attr_64), np.zeros((epad, R), np.float32)])
    weights = np.concatenate([np.asarray(L1_gnn_Wi)[None], np.asarray(L1_gnn_Wj)[None], np.asarray(L1_gnn_res_W1),
                              np.asarray(L1_gnn_res_W2), np.asarray(L1_gnn_Wv)[None]])
    cols = np.concatenate([np.asarray(L1_gnn_bi)[None], np.asarray(L1_gnn_res_b1), np.asarray(L1_gnn_res_b2),
                           np.asarray(L1_gnn_bv)[None], np.asarray(L1_gnn_gate)[None]])
    arrays = {
        "x": np.concatenate([np.asarray(x), np.zeros((nrows - n, P), np.float32)]),
        "src_col": src.reshape(tiles, P).T, "dst_col": dst.reshape(tiles, P).T,
        "src_row": src.reshape(P, tiles), "dst_row": dst.reshape(P, tiles),
        "attr_t": attr.T,
        "WgT": np.asarray(L1_gnn_Wg).T,
        "WT": weights.transpose(2, 0, 1),
        "cols": cols.T,
        "bj": np.asarray(L1_gnn_bj)[None],
    }
    arrays = {f"in_{k}": np.ascontiguousarray(a) for k, a in arrays.items()}
    nc = bacc.Bacc("TRN2", target_bir_lowering=False, num_devices=1)
    ins = {k[3:]: nc.dram_tensor(k, a.shape, mybir.dt.from_np(a.dtype), kind="ExternalInput").ap()
           for k, a in arrays.items()}
    out = nc.dram_tensor("out_0", [nrows, P], F32, kind="ExternalOutput").ap()
    gnn_kernel(nc, n, ins, out)
    r = run_bass_kernel_spmd(nc, [arrays], core_ids=[0])
    return r.results[0]["out_0"][:n]
```

```python
from contextlib import ExitStack

import concourse.bass as bass
from concourse import mybir

P = 128
GT = 4
CG = 6
CT = GT * CG
GE = GT * P
CE = CT * P
ACCS = 8
NB = 512
LAG = 3
R = 64

F32 = mybir.dt.float32
BF16 = mybir.dt.bfloat16
I32 = mybir.dt.int32
ALU = mybir.AluOpType
ACT = mybir.ActivationFunctionType


def sizes(n_nodes, n_edges):
    chunks = -(-n_edges // CE)
    blocks = 2 * -(-(n_nodes + 1 + 2 * P) // (2 * NB))
    return chunks, blocks * NB


def gnn_kernel(nc, n_nodes, ins, out):
    T = ins["src_col"].shape[1]
    CH = T // CT
    NROWS = ins["x"].shape[0]
    NT = NROWS // P
    BLOCKS = NROWS // NB
    SPARE = NROWS - P
    EPAD = T * P
    HIS = NT
    ZEROS = NROWS // 8

    ctx = ExitStack()
    with ctx:
        def dram(name, shape, dt):
            return nc.dram_tensor(name, shape, dt, kind="Internal").ap()

        y_tab = dram("y_tab", [NROWS, P], F32)
        v_tab = dram("v_tab", [NROWS, P], F32)
        x1_tab = dram("x1_tab", [NROWS, P], F32)
        xT_tab = dram("xT_tab", [P, NROWS], F32)
        uT_tab = dram("uT_tab", [P, NROWS], F32)
        rows_tab = dram("rows_tab", [2, 2, EPAD], BF16)
        conv_acc = [dram(f"conv_acc{q}", [NROWS, P], F32) for q in range(ACCS)]
        pair_acc = [dram(f"pair_acc{q}", [NROWS, P], F32) for q in range(ACCS)]

        stage = [ctx]
        held = []

        def sb(name, shape, dt=F32):
            return stage[-1].enter_context(nc.sbuf_tensor(name, shape, dt))

        def ps(name, shape, dt=F32):
            return stage[-1].enter_context(nc.psum_tensor(name, shape, dt))

        def sem(name):
            held.append(nc.alloc_semaphore(name))
            return held[-1]

        def end_stage():
            stage.pop()
            nc.clear_and_free_semaphores(held[:])
            nc.all_engine_barrier()
            held.clear()

        src_f = sb("src_f", [P, T])
        dst_f = sb("dst_f", [P, T])
        ident = sb("ident", [P, P])
        not_earlier = sb("not_earlier", [P, P])
        spare_row = sb("spare_row", [P, 1])
        hilo_w = sb("hilo_w", [2, P], BF16)
        ones_row = sb("ones_row", [1, P])
        dis = sb("dis", [P, NT])
        iota = sb("iota", [P, P])
        in_window = sb("in_window", [P, T])
        base_p = sb("base_p", [P, CH])
        base_i = sb("base_i", [1, CH], I32)
        fits = sb("fits", [1, 1], I32)
        zeros = sb("zeros", [P, ZEROS])

        with ExitStack() as s:
            stage.append(s)
            NG = T // 8
            src_i = sb("src_i", [P, T], I32)
            dst_i = sb("dst_i", [P, T], I32)
            rows_i = sb("rows_i", [P, 2, T], I32)
            part_i = sb("part_i", [P, 2, T], I32)
            rows_b = sb("rows_b", [P, 2, 2, T], BF16)
            dst_hi = sb("dst_hi", [P, T])
            dst_lo = sb("dst_lo", [P, T])
            iota_i = sb("iota_i", [P, P], I32)
            row_i = sb("row_i", [P, 1], I32)
            hi_w = sb("hi_w", [2, 1])
            hi_hot = sb("hi_hot", [P, 2, 8, HIS], BF16)
            lo_hot = sb("lo_hot", [P, 2, 8, P], BF16)
            deg_ps = ps("deg_ps", [P, HIS])
            first_p = sb("first_p", [P, P])
            part_p = sb("part_p", [P, 1])
            base = sb("base", [P, CH])
            reach = sb("reach", [P, 2])
            within = sb("within", [P, 2])
            both = sb("both", [P, 1])
            ones_col = sb("ones_col", [P, 1])
            base_ps = ps("base_ps", [P, CH])
            fits_ps = ps("fits_ps", [P, 1])
            cast, based, compared, fitted = sem("cast"), sem("based"), sem("compared"), sem("fitted")
            win_own = sem("win_own")
            deg = sb("deg", [P, NT])
            degc = sb("degc", [P, NT])
            half = sb("half", [P, NT])
            rsq = sb("rsq", [P, NT])
            cols_in, rows_in, dve_own, iota_made = sem("cols_in"), sem("rows_in"), sem("dve_own"), sem("iota_made")
            rows_made, rows_out, hots, hots_used = sem("rows_made"), sem("rows_out"), sem("hots"), sem("hots_used")
            pool_own, tri_made, clamped, rooted = sem("pool_own"), sem("tri_made"), sem("clamped"), sem("rooted")
            mm_zero, zeros_made, dis_made, cleared = sem("mm_zero"), sem("zeros_made"), sem("dis_made"), sem("cleared")

            with nc.Block() as block:
                @block.sync
                def _(sp):
                    sp.dma_start(dst_i[:, :], ins["dst_col"]).then_inc(cols_in, 16)
                    sp.dma_start(src_i[:, :], ins["src_col"]).then_inc(cols_in, 16)
                    sp.dma_start(rows_i[:, 0, :], ins["src_row"]).then_inc(rows_in, 16)
                    sp.dma_start(rows_i[:, 1, :], ins["dst_row"]).then_inc(rows_in, 16)
                    sp.wait_ge(rows_made, 1)
                    for k in range(2):
                        for s_ in range(2):
                            sp.dma_start(rows_tab[k, s_, :].rearrange("(p t) -> p t", t=T),
                                         rows_b[:, k, s_, :]).then_inc(rows_out, 16)
                    sp.wait_ge(rows_out, 64)

                @block.gpsimd
                def _(pool):
                    pool.iota(iota_i[:, :], [[1, P]], base=0, channel_multiplier=0).then_inc(iota_made, 1)
                    pool.iota(row_i[:, :], [[0, 1]], base=SPARE, channel_multiplier=1).then_inc(iota_made, 1)
                    pool.memset(ident[:, :], 0.0).then_inc(pool_own, 1)
                    pool.memset(not_earlier[:, :], 1.0).then_inc(pool_own, 1)
                    pool.memset(hi_w[:, :], 1.0).then_inc(pool_own, 1)
                    pool.wait_ge(pool_own, 3)
                    pool.affine_select(out=ident[:, :], in_=ident[:, :], compare_op=ALU.not_equal, fill=1.0,
                                       base=0, pattern=[[-1, P]], channel_multiplier=1).then_inc(tri_made, 1)
                    pool.affine_select(out=not_earlier[:, :], in_=not_earlier[:, :], compare_op=ALU.is_ge,
                                       fill=0.0, base=0, pattern=[[-1, P]],
                                       channel_multiplier=1).then_inc(tri_made, 1)
                    pool.affine_select(out=hi_w[:, :], in_=hi_w[:, :], compare_op=ALU.not_equal, fill=128.0,
                                       base=0, pattern=[[0, 1]], channel_multiplier=1).then_inc(tri_made, 1)
                    pool.wait_ge(clamped, 2)
                    pool.tensor_tensor(rsq[:, :], degc[:, :], half[:, :], ALU.pow).then_inc(rooted, 1)

                @block.vector
                def _(dve):
                    dve.memset(zeros[:, :], 0.0)
                    dve.memset(half[:, :], -0.5)
                    dve.memset(ones_col[:, :], 1.0)
                    dve.memset(first_p[:, :], 0.0).then_inc(win_own, 1)
                    dve.wait_ge(win_own, 1)
                    dve.memset(first_p[0:1, :], 1.0)
                    dve.memset(ones_row[:, :], 1.0)
                    dve.memset(hilo_w[:, :], 1.0).then_inc(zeros_made, 1)
                    dve.wait_ge(iota_made, 2)
                    dve.tensor_copy(iota[:, :], iota_i[:, :])
                    dve.tensor_copy(spare_row[:, :], row_i[:, :]).then_inc(win_own, 1)
                    dve.wait_ge(cols_in, 32)
                    dve.tensor_scalar(part_i[:, 0, :], dst_i[:, :], 7, None, ALU.arith_shift_right)
                    dve.tensor_scalar(part_i[:, 1, :], dst_i[:, :], 127, None, ALU.bitwise_and).then_inc(dve_own, 1)
                    dve.tensor_copy(dst_f[:, :], dst_i[:, :])
                    dve.wait_ge(win_own, 2)
                    dve.tensor_scalar(part_p[:, :], spare_row[:, :], -float(SPARE), None, ALU.add)
                    dve.tensor_copy(src_f[:, :], src_i[:, :]).then_inc(cast, 1)
                    dve.wait_ge(dve_own, 1)
                    dve.tensor_copy(dst_hi[:, :], part_i[:, 0, :])
                    dve.tensor_copy(dst_lo[:, :], part_i[:, 1, :]).then_inc(dve_own, 1)
                    dve.wait_ge(dve_own, 2)

                    def one_hots(par, t):
                        dve.tensor_tensor(lo_hot[:, par, :, :],
                                          iota[:, :].unsqueeze(1).to_broadcast([P, 8, P]),
                                          dst_lo[:, bass.ds(t, 8)].unsqueeze(2).to_broadcast([P, 8, P]), ALU.is_equal)
                        return dve.tensor_tensor(hi_hot[:, par, :, :],
                                                 iota[:, 0:HIS].unsqueeze(1).to_broadcast([P, 8, HIS]),
                                                 dst_hi[:, bass.ds(t, 8)].unsqueeze(2).to_broadcast([P, 8, HIS]),
                                                 ALU.is_equal)

                    with dve.Fori(0, NG // 2) as i:
                        for par in range(2):
                            dve.wait_ge(hots_used, 2 * i + par + 1)
                            one_hots(par, (2 * i + par) * 8).then_inc(hots, 1)
                    if NG % 2:
                        dve.wait_ge(hots_used, NG)
                        one_hots(0, (NG - 1) * 8).then_inc(hots, 1)

                    dve.wait_ge(based, 1)
                    dve.tensor_copy(base[:, :], base_ps[:, :]).then_inc(win_own, 1)
                    dve.wait_ge(win_own, 3)
                    dve.tensor_copy(base_i[:, :], base[0:1, :])
                    dve.tensor_scalar(base_p[:, :], base[:, :], part_p[:, 0:1], None, ALU.add)
                    dve.tensor_tensor(in_window[:, :].rearrange("p (c t) -> p c t", t=CT),
                                      dst_f[:, :].rearrange("p (c t) -> p c t", t=CT),
                                      base[:, :].unsqueeze(2).to_broadcast([P, CH, CT]), ALU.subtract
                                      ).then_inc(win_own, 1)
                    dve.wait_ge(win_own, 4)
                    dve.tensor_reduce(reach[:, 0:1], in_window[:, :], mybir.AxisListType.X, ALU.min)
                    dve.tensor_reduce(reach[:, 1:2], in_window[:, :], mybir.AxisListType.X, ALU.max
                                      ).then_inc(win_own, 1)
                    dve.wait_ge(win_own, 5)
                    dve.tensor_scalar(within[:, 0:1], reach[:, 0:1], 0.0, None, ALU.is_ge)
                    dve.tensor_scalar(within[:, 1:2], reach[:, 1:2], float(P), None, ALU.is_lt).then_inc(win_own, 1)
                    dve.wait_ge(win_own, 6)
                    dve.tensor_tensor(both[:, :], within[:, 0:1], within[:, 1:2], ALU.mult).then_inc(compared, 1)
                    dve.wait_ge(fitted, 1)
                    dve.tensor_copy(fits[:, :], fits_ps[0:1, :])

                    dve.wait_ge(rows_in, 32)
                    dve.tensor_scalar(part_i[:, :, :], rows_i[:, :, :], 7, None, ALU.arith_shift_right).then_inc(dve_own, 1)
                    dve.wait_ge(dve_own, 3)
                    dve.tensor_copy(rows_b[:, 0, :, :], part_i[:, :, :]).then_inc(dve_own, 1)
                    dve.wait_ge(dve_own, 4)
                    dve.tensor_scalar(part_i[:, :, :], rows_i[:, :, :], 127, None, ALU.bitwise_and).then_inc(dve_own, 1)
                    dve.wait_ge(dve_own, 5)
                    dve.tensor_copy(rows_b[:, 1, :, :], part_i[:, :, :]).then_inc(rows_made, 1)
                    dve.wait_ge(tri_made, 3)
                    dve.tensor_scalar(hilo_w[:, :], hilo_w[:, :], hi_w[:, 0:1], None, ALU.mult)

                    dve.wait_ge(hots_used, NG + 3)
                    dve.tensor_copy(deg[:, :], deg_ps[:, 0:NT]).then_inc(dve_own, 1)
                    dve.wait_ge(dve_own, 6)
                    dve.tensor_scalar(degc[:, :], deg[:, :], 1.0, None, ALU.max).then_inc(clamped, 2)
                    dve.wait_ge(rooted, 1)
                    dve.scalar_tensor_tensor(out=dis[:, :], in0=deg[:, :], scalar=0.0, in1=rsq[:, :],
                                             op0=ALU.is_gt, op1=ALU.mult).then_inc(dis_made, 1)

                @block.tensor
                def _(pe):
                    pe.sem_inc(hots_used, 2)
                    pe.wait_ge(zeros_made, 1)
                    pe.wait_ge(cast, 1)
                    pe.matmul(base_ps[:, :], first_p[:, :],
                              dst_f[:, :].rearrange("p (c t) -> p c t", t=CT)[:, :, 0], start=True, stop=True
                              ).then_inc(based, 1)
                    zb = zeros[:, 0:P]
                    pe.matmul(deg_ps[:, :], zb, zeros[:, 0:HIS], start=True, stop=False)

                    def count(par):
                        for k in range(8):
                            m = pe.matmul(deg_ps[:, :], lo_hot[:, par, k, :], hi_hot[:, par, k, :],
                                          start=False, stop=False)
                        m.then_inc(hots_used, 1)

                    with pe.Fori(0, NG // 2) as i:
                        for par in range(2):
                            pe.wait_ge(hots, 2 * i + par + 1)
                            count(par)
                    if NG % 2:
                        pe.wait_ge(hots, NG)
                        count(0)
                    pe.matmul(deg_ps[:, :], zb, zeros[:, 0:HIS], start=False, stop=True).then_inc(hots_used, 1)
                    pe.wait_ge(compared, 1)
                    pe.matmul(fits_ps[0:1, :], both[:, :], ones_col[:, :], start=True, stop=True).then_inc(fitted, 1)
            end_stage()

        with ExitStack() as s:
            stage.append(s)
            xs = sb("xs", [P, NT, P])
            x_in, y_made, y_out = sem("x_in"), sem("y_made"), sem("y_out")
            with nc.Block() as block:
                @block.sync
                def _(sp):
                    sp.dma_start(xs[:, :, :], ins["x"].rearrange("(t p) f -> p t f", p=P)).then_inc(x_in, 16)
                    sp.wait_ge(y_made, 1)
                    sp.dma_start(y_tab.rearrange("(t p) f -> p t f", p=P), xs[:, :, :]).then_inc(y_out, 16)
                    sp.wait_ge(y_out, 16)

                @block.vector
                def _(dve):
                    dve.wait_ge(x_in, 16)
                    dve.tensor_tensor(xs[:, :, :], xs[:, :, :], dis[:, :].unsqueeze(2).to_broadcast([P, NT, P]),
                                      ALU.mult).then_inc(y_made, 1)
            end_stage()

        def fits_here(eng):
            return eng.value_load(fits[0:1, 0:1], min_val=0, max_val=P) == P

        def done(c, g, before=0):
            return c * CG + (g + CG + 1 - before)

        def window_done(c, before=0):
            return c + (CG + 1 - before)

        def scatter_buffers(tag, edge_product):
            b = {}
            if edge_product:
                b["wg"] = sb(tag + "wg", [R, P])
                b["attr"] = sb(tag + "attr", [R, CG, GE])
                b["prod"] = sb(tag + "prod", [P, 2, GE])
                b["filt_ps"] = ps(tag + "filt_ps", [P, 2, GE])
                b["window_in"] = sb(tag + "window_in", [P, P])
                b["window"] = sb(tag + "window", [P, P])
                b["hot"] = sb(tag + "hot", [P, 2, GE])
                b["values"] = sb(tag + "values", [P, 2, GE])
                b["wrows_ps"] = ps(tag + "wrows_ps", [P, GE])
                b["values_ps"] = ps(tag + "values_ps", [P, GE])
                b["wbase"] = sb(tag + "wbase", [P, 1])
            b["rows"] = sb(tag + "rows", [2, CG, 2, GE], BF16)
            b["gidx"] = sb(tag + "gidx", [P, CG, GT], I32)
            b["got"] = sb(tag + "got", [P, CG, GE])
            b["tcol"] = sb(tag + "tcol", [P, CT])
            b["same"] = sb(tag + "same", [P, 2, GE])
            b["earlier"] = sb(tag + "earlier", [P, 2, GT])
            b["shifted"] = sb(tag + "shifted", [P, CT])
            b["pick"] = sb(tag + "pick", [P, 2, GT])
            b["sidx"] = sb(tag + "sidx", [P, CG, GT], I32)
            b["summed"] = sb(tag + "summed", [P, CG, GE])
            b["rows_ps"] = ps(tag + "rows_ps", [P, 2, GE])
            b["sum_ps"] = ps(tag + "sum_ps", [P, 2, GE])
            for name in ("rows_in", "attr_in", "got_in"):
                b[name] = [sem(f"{tag}_{name}{g}") for g in range(CG)]
            b["acc_done"] = [sem(f"{tag}_acc_done{q}") for q in range(ACCS)]
            for name in ("w_in", "copies_cleared", "rows_made", "same_made", "counted", "columns", "filt_made", "prod_made",
                         "sums_made", "sums_out", "sidx_made", "gidx_made", "gather_passed", "scatter_passed",
                         "sync_passed", "window_ready", "window_taken", "window_set", "hot_made", "looked_up",
                         "values_out"):
                b[name] = sem(f"{tag}_{name}")
            return b

        def scatter_pass(b, table, gather_f, target, target_f, acc, edge_product, window):
            rows, gidx, got, tcol, same = b["rows"], b["gidx"], b["got"], b["tcol"], b["same"]
            earlier, shifted, pick, sidx, summed = b["earlier"], b["shifted"], b["pick"], b["sidx"], b["summed"]
            rows_ps, sum_ps = b["rows_ps"], b["sum_ps"]
            if edge_product:
                wg, attr, prod, filt_ps = b["wg"], b["attr"], b["prod"], b["filt_ps"]
            if window:
                window_in, window_sb, hot, values = b["window_in"], b["window"], b["hot"], b["values"]
                wrows_ps, values_ps, wbase = b["wrows_ps"], b["values_ps"], b["wbase"]
            acc_done = b["acc_done"]

            def sync(sp):
                if edge_product:
                    sp.dma_start(wg[:, :], ins["WgT"]).then_inc(b["w_in"], 16)
                with sp.Fori(0, CH) as c:
                    if window:
                        base = sp.value_load(base_i[0:1, bass.ds(c, 1)], min_val=0, max_val=NROWS - P)
                        sp.wait_ge(b["window_taken"], c + 1)
                        sp.sem_inc(b["sync_passed"], 1)
                        sp.dma_start(window_in[:, :], table[bass.ds(base, P), :]).then_inc(b["window_ready"], 16)
                    for g in range(CG):
                        sp.wait_ge(b["rows_made"], done(c, g, CG))
                        sp.sem_inc(b["sync_passed"], 1)
                        sp.dma_start(rows[:, g, :, :], rows_tab[:, :, bass.ds(c * CE + g * GE, GE)]
                                     ).then_inc(b["rows_in"][g], 16)
                        if edge_product:
                            sp.wait_ge(b["filt_made"], done(c, g, CG))
                            sp.sem_inc(b["sync_passed"], 1)
                            sp.dma_start(attr[:, g, :], ins["attr_t"][:, bass.ds(c * CE + g * GE, GE)]
                                         ).then_inc(b["attr_in"][g], 16)

            def gpsimd(pool):
                def gather(c, g):
                    pool.wait_ge(b["gidx_made"], done(c, g))
                    pool.wait_ge(b["prod_made" if edge_product else "sums_made"], done(c, g, CG))
                    pool.sem_inc(b["gather_passed"], 1)
                    for k in range(GT):
                        pool.indirect_dma_start(
                            out=got[:, g, k * P:(k + 1) * P], out_offset=None, in_=table,
                            in_offset=bass.IndirectOffsetOnAxis(ap=gidx[:, g, k:k + 1], axis=0)
                        ).then_inc(b["got_in"][g], 16)

                def scatter(c, g, first):
                    pool.wait_ge(b["sums_out"], done(c, g))
                    pool.wait_ge(b["sidx_made"], done(c, g))
                    for k in range(GT):
                        t = g * GT + k
                        q = t % ACCS
                        if not (first and t < ACCS):
                            pool.wait_ge(acc_done[q], c * (CT // ACCS * 16) + (t // ACCS) * 16)
                        pool.sem_inc(b["scatter_passed"], 1)
                        pool.indirect_dma_start(
                            out=acc[q], out_offset=bass.IndirectOffsetOnAxis(ap=sidx[:, g, k:k + 1], axis=0),
                            in_=summed[:, g, k * P:(k + 1) * P], in_offset=None, compute_op=ALU.add
                        ).then_inc(acc_done[q], 16)

                def chunk(c, first, last):
                    for g in range(CG):
                        if not window:
                            if g + LAG < CG:
                                gather(c, g + LAG)
                            elif not last:
                                gather(c + 1, g + LAG - CG)
                        scatter(c, g, first)

                pool.sem_inc(b["scatter_passed"], CT)
                if not window:
                    for g in range(LAG):
                        gather(0, g)
                chunk(0, True, CH == 1)
                if CH > 2:
                    with pool.Fori(1, CH - 1) as c:
                        chunk(c, False, False)
                if CH > 1:
                    chunk(CH - 1, False, True)
                for q in range(ACCS):
                    pool.wait_ge(acc_done[q], CH * (CT // ACCS) * 16)

            def tensor(pe):
                pe.sem_inc(b["rows_made"], CG)
                pe.sem_inc(b["filt_made"], CG)
                pe.sem_inc(b["sums_made"], CG)
                pe.sem_inc(b["looked_up"], CG)
                if edge_product:
                    pe.wait_ge(b["w_in"], 16)

                def front(c, g):
                    h = g % 2
                    pe.wait_ge(b["rows_in"][g], c * 16 + 16)
                    if window:
                        pe.wait_ge(b["hot_made"], done(c, g, 1))
                        pe.matmul(wrows_ps[:, :], hilo_w[:, :], rows[:, g, 1 - target, :], start=True, stop=True)
                    pe.wait_ge(b["same_made"], done(c, g, 2))
                    pe.matmul(rows_ps[:, h, :], hilo_w[:, :], rows[:, g, target, :], start=True, stop=True
                              ).then_inc(b["rows_made"], 1)
                    if edge_product:
                        pe.wait_ge(b["attr_in"][g], c * 16 + 16)
                        pe.wait_ge(b["prod_made"], done(c, g, 2))
                        for k in range(GT):
                            col = slice(k * P, (k + 1) * P)
                            m = pe.matmul(filt_ps[:, h, col], attr[:, g, col], wg[:, :], start=True, stop=True)
                        m.then_inc(b["filt_made"], 1)

                def look_up(c, g):
                    h = g % 2
                    pe.wait_ge(b["window_set"], c + 1)
                    pe.wait_ge(b["hot_made"], done(c, g))
                    pe.wait_ge(b["values_out"], done(c, g, 1))
                    for k in range(GT):
                        col = slice(k * P, (k + 1) * P)
                        m = pe.matmul(values_ps[:, col], hot[:, h, col], window_sb[:, :], start=True, stop=True)
                    m.then_inc(b["looked_up"], 1)

                def back(c, g):
                    h = g % 2
                    pe.wait_ge(b["same_made"], done(c, g))
                    pe.wait_ge(b["sums_out"], done(c, g, 2))
                    if edge_product:
                        pe.wait_ge(b["prod_made"], done(c, g))
                        terms = prod[:, h, :]
                    else:
                        pe.wait_ge(b["got_in"][g], c * (GT * 16) + GT * 16)
                        terms = got[:, g, :]
                    for k in range(GT):
                        col = slice(k * P, (k + 1) * P)
                        m = pe.matmul(sum_ps[:, h, col], same[:, h, col], terms[:, col], start=True, stop=True)
                    m.then_inc(b["sums_made"], 1)

                def chunk(c, last):
                    for g in range(CG):
                        nxt = (c, g + 1) if g + 1 < CG else None if last else (c + 1, 0)
                        if nxt:
                            front(*nxt)
                        back(c, g)
                        if nxt and window:
                            look_up(*nxt)

                front(0, 0)
                if window:
                    look_up(0, 0)
                with pe.Fori(0, CH - 1) as c:
                    chunk(c, False)
                chunk(CH - 1, True)

            def vector(dve):
                dve.sem_inc(b["same_made"], CG)
                dve.sem_inc(b["prod_made"], CG)
                dve.sem_inc(b["gidx_made"], CG)
                dve.sem_inc(b["hot_made"], CG)
                if not window:
                    for g in range(CG):
                        dve.tensor_copy(gidx[:, g, :], gather_f[:, g * GT:(g + 1) * GT]).then_inc(b["gidx_made"], 1)

                def chunk(c, last):
                    if window:
                        dve.tensor_copy(wbase[:, :], base_p[:, bass.ds(c, 1)])
                    dve.tensor_copy(tcol[:, :], target_f[:, bass.ds(c * CT, CT)]).then_inc(b["columns"], 1)
                    dve.wait_ge(b["columns"], c * 2 + 1)
                    dve.tensor_scalar(shifted[:, :], tcol[:, :], spare_row[:, 0:1], None,
                                      ALU.subtract).then_inc(b["columns"], 1)
                    dve.wait_ge(b["columns"], c * 2 + 2)
                    for g in range(CG):
                        h = g % 2
                        dve.wait_ge(b["rows_made"], done(c, g))
                        if window:
                            dve.wait_ge(b["looked_up"], done(c, g, 2))
                            dve.tensor_scalar(hot[:, h, :], wrows_ps[:, :], wbase[:, 0:1], None, ALU.is_equal
                                              ).then_inc(b["hot_made"], 1)
                        dve.wait_ge(b["sums_made"], done(c, g, 2))
                        for k in range(GT):
                            col = slice(k * P, (k + 1) * P)
                            t = g * GT + k
                            m = dve.scalar_tensor_tensor(
                                out=same[:, h, col], in0=rows_ps[:, h, col], scalar=tcol[:, t:t + 1],
                                in1=not_earlier[:, :], op0=ALU.is_equal, op1=ALU.mult,
                                accum_out=earlier[:, h, k:k + 1])
                        m.then_inc(b["counted"], 1)
                        dve.wait_ge(b["counted"], c * CG + (g + 1))
                        dve.wait_ge(b["sidx_made"], done(c, g, 2))
                        dve.scalar_tensor_tensor(
                            out=pick[:, h, :], in0=earlier[:, h, :], scalar=1.5,
                            in1=shifted[:, g * GT:(g + 1) * GT], op0=ALU.is_lt, op1=ALU.mult
                        ).then_inc(b["same_made"], 1)
                        if not window and (edge_product or not last):
                            dve.wait_ge(b["got_in"][g], c * (GT * 16) + GT * 16)
                        if edge_product:
                            dve.wait_ge(b["filt_made"], done(c, g))
                            if window:
                                dve.wait_ge(b["values_out"], done(c, g))
                            terms = values[:, h, :] if window else got[:, g, :]
                            dve.tensor_tensor(prod[:, h, :], filt_ps[:, h, :], terms, ALU.mult
                                              ).then_inc(b["prod_made"], 1)
                        if not window and not last:
                            dve.tensor_copy(gidx[:, g, :], gather_f[:, bass.ds(c * CT + (CT + g * GT), GT)]
                                            ).then_inc(b["gidx_made"], 1)

                with dve.Fori(0, CH - 1) as c:
                    chunk(c, False)
                chunk(CH - 1, True)

            def scalar(act):
                act.sem_inc(b["sums_out"], CG)
                act.sem_inc(b["sidx_made"], CG)
                act.sem_inc(b["values_out"], CG)
                act.sem_inc(b["window_taken"], 1)
                with act.Fori(0, CH) as c:
                    for g in range(CG):
                        h = g % 2
                        if window:
                            if g == 0:
                                act.wait_ge(b["window_ready"], c * 16 + 16)
                                act.wait_ge(b["looked_up"], done(c, g, 1))
                                act.copy(window_sb[:, :], window_in[:, :]).then_inc(b["window_set"], 1)
                                act.wait_ge(b["window_set"], c + 1)
                                act.sem_inc(b["window_taken"], 1)
                            act.wait_ge(b["looked_up"], done(c, g))
                            act.wait_ge(b["prod_made"], done(c, g, 2))
                            act.copy(values[:, h, :], values_ps[:, :]).then_inc(b["values_out"], 1)
                        act.wait_ge(b["scatter_passed"], c * CT + (g * GT + GT + ACCS))
                        act.wait_ge(b["same_made"], done(c, g))
                        act.activation(sidx[:, g, :], pick[:, h, :], ACT.Identity,
                                       bias=spare_row[:, 0:1]).then_inc(b["sidx_made"], 1)
                        act.wait_ge(b["sums_made"], done(c, g))
                        act.copy(summed[:, g, :], sum_ps[:, h, :]).then_inc(b["sums_out"], 1)

            return sync, gpsimd, tensor, vector, scalar

        with ExitStack() as s:
            stage.append(s)
            b = scatter_buffers("conv", False)
            any_sync, any_pool, any_pe, any_dve, any_act = scatter_pass(
                b, y_tab, src_f, 1, dst_f, conv_acc, False, False)
            win_ps = ps("win_ps", [P, P])
            win = sb("win", [P, P])
            widx = sb("widx", [P, 1], I32)
            rcol = sb("rcol", [P, CT])
            win_sums, win_out, win_added, merged = sem("win_sums"), sem("win_out"), sem("win_added"), sem("merged")
            pair_cleared = sem("pair_acc_cleared")

            with nc.Block() as block:
                @block.sync
                def _(sp):
                    for q in range(ACCS):
                        sp.dma_start(pair_acc[q].rearrange("(p a) f -> p (a f)", p=P),
                                     zeros[:, :].unsqueeze(1).to_broadcast([P, NROWS // ZEROS, ZEROS])
                                     ).then_inc(pair_cleared, 16)
                    with sp.If(fits_here(sp)):
                        sp.wait_ge(pair_cleared, ACCS * 16)
                    with sp.Else():
                        any_sync(sp)
                        sp.wait_ge(pair_cleared, ACCS * 16)

                @block.gpsimd
                def _(pool):
                    def gather(c, g):
                        pool.wait_ge(b["gidx_made"], done(c, g))
                        pool.wait_ge(b["sums_made"], done(c, g, CG))
                        pool.sem_inc(b["gather_passed"], 1)
                        for k in range(GT):
                            pool.indirect_dma_start(
                                out=b["got"][:, g, k * P:(k + 1) * P], out_offset=None, in_=y_tab,
                                in_offset=bass.IndirectOffsetOnAxis(ap=b["gidx"][:, g, k:k + 1], axis=0)
                            ).then_inc(b["got_in"][g], 16)

                    def add_window(c):
                        pool.wait_ge(win_out, window_done(c))
                        pool.wait_ge(win_added, c * 16 + 16)
                        pool.sem_inc(b["scatter_passed"], 1)
                        pool.indirect_dma_start(
                            out=conv_acc[0], out_offset=bass.IndirectOffsetOnAxis(ap=widx[:, 0:1], axis=0),
                            in_=win[:, :], in_offset=None, compute_op=ALU.add).then_inc(win_added, 16)

                    def clear(q, to):
                        pool.dma_start(conv_acc[q].rearrange("(p a) f -> p (a f)", p=P),
                                       zeros[:, :].unsqueeze(1).to_broadcast([P, NROWS // ZEROS, ZEROS])
                                       ).then_inc(to, 16)

                    with pool.If(fits_here(pool)):
                        clear(0, win_added)
                        for g in range(CG):
                            gather(0, g)
                        with pool.Fori(1, CH) as c:
                            for g in range(CG):
                                gather(c, g)
                                if g == 2:
                                    add_window(c - 1)
                        add_window(CH - 1)
                        pool.wait_ge(win_added, CH * 16 + 16)
                    with pool.Else():
                        for q in range(ACCS):
                            clear(q, b["copies_cleared"])
                        pool.wait_ge(b["copies_cleared"], ACCS * 16)
                        any_pool(pool)
                        for q in range(1, ACCS):
                            pool.dma_start(conv_acc[0].rearrange("(p a) f -> p (a f)", p=P),
                                           conv_acc[q].rearrange("(p a) f -> p (a f)", p=P),
                                           accum_op=ALU.add, max_dma_last_dim=4 * 2048).then_inc(merged, 16)
                            pool.wait_ge(merged, q * 16)

                @block.tensor
                def _(pe):
                    with pe.If(fits_here(pe)):
                        pe.sem_inc(b["sums_made"], CG)
                        with pe.Fori(0, CH) as c:
                            for g in range(CG):
                                h = g % 2
                                pe.wait_ge(b["hot_made"], done(c, g))
                                pe.wait_ge(b["got_in"][g], c * (GT * 16) + GT * 16)
                                if g == 0:
                                    pe.wait_ge(win_out, window_done(c, 1))
                                for k in range(GT):
                                    col = slice(k * P, (k + 1) * P)
                                    m = pe.matmul(win_ps[:, :], b["same"][:, h, col], b["got"][:, g, col],
                                                  start=g == 0 and k == 0, stop=g == CG - 1 and k == GT - 1)
                                m.then_inc(b["sums_made"], 1)
                    with pe.Else():
                        any_pe(pe)

                @block.vector
                def _(dve):
                    with dve.If(fits_here(dve)):
                        dve.sem_inc(b["gidx_made"], CG)
                        dve.sem_inc(b["hot_made"], CG)
                        for g in range(CG):
                            dve.tensor_copy(b["gidx"][:, g, :], src_f[:, g * GT:(g + 1) * GT]
                                            ).then_inc(b["gidx_made"], 1)

                        def chunk(c, last):
                            dve.wait_ge(b["hot_made"], done(c, 0, 1))
                            dve.tensor_copy(rcol[:, :], in_window[:, bass.ds(c * CT, CT)]).then_inc(b["columns"], 1)
                            dve.wait_ge(b["columns"], c + 1)
                            for g in range(CG):
                                h = g % 2
                                dve.wait_ge(b["sums_made"], done(c, g, 2))
                                for k in range(GT):
                                    t = g * GT + k
                                    m = dve.tensor_scalar(b["same"][:, h, k * P:(k + 1) * P], iota[:, :],
                                                          rcol[:, t:t + 1], None, ALU.is_equal)
                                m.then_inc(b["hot_made"], 1)
                                if not last:
                                    dve.wait_ge(b["got_in"][g], c * (GT * 16) + GT * 16)
                                    dve.tensor_copy(b["gidx"][:, g, :], src_f[:, bass.ds(c * CT + (CT + g * GT), GT)]
                                                    ).then_inc(b["gidx_made"], 1)

                        with dve.Fori(0, CH - 1) as c:
                            chunk(c, False)
                        chunk(CH - 1, True)
                    with dve.Else():
                        any_dve(dve)

                @block.scalar
                def _(act):
                    with act.If(fits_here(act)):
                        act.sem_inc(win_out, CG)
                        with act.Fori(0, CH) as c:
                            act.wait_ge(b["sums_made"], done(c, CG - 1))
                            act.wait_ge(win_added, c * 16 + 16)
                            act.copy(widx[:, :], base_p[:, bass.ds(c, 1)])
                            act.copy(win[:, :], win_ps[:, :]).then_inc(win_out, 1)
                    with act.Else():
                        any_act(act)
            end_stage()

        WI, WJ, W1, W2, WV = 0, 1, 2, 5, 8
        BI, B1, B2, BV, GATE = 0, 1, 4, 7, 8
        CAP = 40.0
        EPS = 1e-5
        PAIRS = BLOCKS // 2

        with ExitStack() as s:
            stage.append(s)
            wts = sb("n1wts", [P, 2, P])
            bi_col = sb("n1bi", [P, 9])
            bj_row = sb("n1bj", [1, P])
            conv = sb("n1conv", [P, 2, NB])
            xin = sb("n1xin", [P, 2, NB])
            hid = sb("n1hid", [P, 2, NB])
            x1 = sb("n1x1", [P, 2, NB])
            xp = sb("n1xp", [P, 2, NB])
            xT = sb("n1xT", [P, 2, NB])
            low = sb("n1low", [P, 2, 2, NB])
            ex = sb("n1ex", [P, 2, 2, NB])
            vu = sb("n1vu", [P, 2, 2, NB])
            stats = sb("n1stats", [P, 2, 4, 6])
            mv = sb("n1mv", [P, 2, 4, 2])
            var = sb("n1var", [P, 2, 4])
            rstd = sb("n1rstd", [P, 2, 4])
            half4 = sb("n1half", [P, 4])
            one_ps = [ps(f"n1one{h}", [P, NB]) for h in range(2)]
            two_ps = [ps(f"n1two{h}", [P, NB]) for h in range(2)]
            names = ("scaled", "joined", "stats", "mv", "var", "rstd", "x1", "low", "ex", "ln", "xp",
                     "xTps", "xT", "vups", "low2", "ex2", "ln2", "vu", "stored")
            sm = {k: sem("n1_" + k) for k in names}
            w_in = sem("n1_w_in")
            sync_passed = sem("n1_sync_passed")
            half_made = sem("n1_half_made")
            loaded = [sem(f"n1_loaded{h}") for h in range(2)]
            stores = [sem(f"n1_stores{h}") for h in range(2)]

            def block_done(n):
                return n + 3

            with nc.Block() as block:
                @block.sync
                def _(sp):
                    sp.dma_start(wts[:, :, :], ins["WT"][:, WI:WI + 2, :]).then_inc(w_in, 16)
                    sp.dma_start(bi_col[:, :], ins["cols"]).then_inc(w_in, 16)
                    sp.dma_start(bj_row[:, :], ins["bj"]).then_inc(w_in, 16)

                    def load(i, h):
                        at = bass.ds(i * (2 * NB) + h * NB, NB)
                        sp.dma_start(conv[:, h, :].rearrange("p (j f) -> p j f", f=P),
                                     conv_acc[0][at, :].rearrange("(j p) f -> p j f", p=P)).then_inc(loaded[h], 16)
                        sp.dma_start(xin[:, h, :].rearrange("p (j f) -> p j f", f=P),
                                     ins["x"][at, :].rearrange("(j p) f -> p j f", p=P)).then_inc(loaded[h], 16)

                    def pair(i, last):
                        for h in range(2):
                            if not last:
                                sp.wait_ge(sm["joined"], i * 2 + h + 1)
                                sp.sem_inc(sync_passed, 1)
                                load(i + 1, h)
                        for h in range(2):
                            at = bass.ds(i * (2 * NB) + h * NB, NB)
                            sp.wait_ge(sm["x1"], i * 2 + h + 1)
                            sp.sem_inc(sync_passed, 1)
                            sp.dma_start(x1_tab[at, :].rearrange("(j p) f -> p j f", p=P),
                                         x1[:, h, :].rearrange("p (j f) -> p j f", f=P)).then_inc(stores[h], 16)
                        for h in range(2):
                            at = bass.ds(i * (2 * NB) + h * NB, NB)
                            sp.wait_ge(sm["xT"], i * 2 + h + 1)
                            sp.sem_inc(sync_passed, 1)
                            sp.dma_start(xT_tab[:, at], xT[:, h, :]).then_inc(stores[h], 16)
                        for h in range(2):
                            at = bass.ds(i * (2 * NB) + h * NB, NB)
                            sp.wait_ge(sm["vu"], block_done(i * 2 + h))
                            sp.sem_inc(sync_passed, 1)
                            sp.dma_start(v_tab[at, :].rearrange("(j p) f -> p j f", p=P),
                                         vu[:, h, 0, :].rearrange("p (j f) -> p j f", f=P)).then_inc(stores[h], 16)
                            sp.dma_start(uT_tab[:, at], vu[:, h, 1, :]).then_inc(stores[h], 16)
                        for h in range(2):
                            sp.wait_ge(stores[h], i * 64 + 64)
                            sp.sem_inc(sm["stored"], 1)

                    sp.sem_inc(sm["stored"], 2)
                    load(0, 0)
                    load(0, 1)
                    if PAIRS > 1:
                        with sp.Fori(0, PAIRS - 1) as i:
                            pair(i, False)
                    pair(PAIRS - 1, True)

                @block.gpsimd
                def _(pool):
                    pool.memset(half4[:, :], -0.5).then_inc(half_made, 1)
                    pool.wait_ge(half_made, 1)
                    with pool.Fori(0, PAIRS) as i:
                        for h in range(2):
                            pool.wait_ge(sm["var"], i * 2 + h + 1)
                            pool.tensor_tensor(rstd[:, h, :], var[:, h, :], half4[:, :], ALU.pow).then_inc(sm["rstd"], 1)

                @block.vector
                def _(dve):
                    dve.sem_inc(sm["vu"], 2)
                    dve.wait_ge(w_in, 48)
                    with dve.Fori(0, PAIRS) as i:
                        for h in range(2):
                            dve.wait_ge(loaded[h], i * 32 + 32)
                            d = dis[:, bass.ds(i * 8 + h * 4, 4)].unsqueeze(2).to_broadcast([P, 4, P])
                            dve.tensor_tensor(hid[:, h, :].rearrange("p (j f) -> p j f", f=P),
                                              conv[:, h, :].rearrange("p (j f) -> p j f", f=P), d,
                                              ALU.mult).then_inc(sm["scaled"], 1)
                        for h in range(2):
                            dve.wait_ge(sm["scaled"], i * 2 + h + 1)
                            dve.scalar_tensor_tensor(out=hid[:, h, :], in0=hid[:, h, :], scalar=0.0, in1=xin[:, h, :],
                                                     op0=ALU.max, op1=ALU.add).then_inc(sm["joined"], 1)
                        for h in range(2):
                            dve.wait_ge(sm["joined"], i * 2 + h + 1)
                            for j in range(4):
                                m = dve.bn_stats(stats[:, h, j, :], hid[:, h, j * P:(j + 1) * P])
                            m.then_inc(sm["stats"], 1)
                        for h in range(2):
                            dve.wait_ge(sm["stats"], 1)
                            dve.wait_ge(sm["stats"], i * 2 + h + 1)
                            for j in range(4):
                                m = dve.bn_aggr(mv[:, h, j, :], stats[:, h, j, :])
                            m.then_inc(sm["mv"], 1)
                        for h in range(2):
                            dve.wait_ge(sm["mv"], i * 2 + h + 1)
                            dve.tensor_scalar(var[:, h, :], mv[:, h, :, 1], EPS, None, ALU.add).then_inc(sm["var"], 1)
                        for h in range(2):
                            dve.wait_ge(sm["rstd"], i * 2 + h + 1)
                            dve.wait_ge(sm["stored"], block_done(i * 2 + h - 2))
                            for j in range(4):
                                col = slice(j * P, (j + 1) * P)
                                m = dve.tensor_scalar(x1[:, h, col], hid[:, h, col], mv[:, h, j, 0:1],
                                                      rstd[:, h, j:j + 1], ALU.subtract, ALU.mult)
                            m.then_inc(sm["x1"], 1)
                        for h in range(2):
                            dve.wait_ge(sm["x1"], i * 2 + h + 1)
                            dve.tensor_scalar(low[:, h, 0, :], x1[:, h, :], CAP, None, ALU.min).then_inc(sm["low"], 1)
                        for h in range(2):
                            dve.wait_ge(sm["ln"], i * 2 + h + 1)
                            dve.tensor_tensor(xp[:, h, :], x1[:, h, :], low[:, h, 0, :], ALU.max).then_inc(sm["xp"], 1)
                        for h in range(2):
                            dve.wait_ge(sm["vups"], i * 2 + h + 1)
                            dve.tensor_scalar(low[:, h, 0, :], two_ps[h][:, :], CAP, None, ALU.min)
                            dve.tensor_scalar(low[:, h, 1, :], one_ps[h][:, :], bi_col[:, BI:BI + 1], CAP, ALU.add,
                                              ALU.min).then_inc(sm["low2"], 1)
                        for h in range(2):
                            dve.wait_ge(sm["ln2"], i * 2 + h + 1)
                            dve.tensor_tensor(vu[:, h, 0, :], two_ps[h][:, :], low[:, h, 0, :], ALU.max)
                            dve.scalar_tensor_tensor(out=vu[:, h, 1, :], in0=one_ps[h][:, :], scalar=bi_col[:, BI:BI + 1],
                                                     in1=low[:, h, 1, :], op0=ALU.add, op1=ALU.max
                                                     ).then_inc(sm["vu"], 1)

                @block.scalar
                def _(act):
                    with act.Fori(0, PAIRS) as i:
                        for h in range(2):
                            act.wait_ge(sm["low"], i * 2 + h + 1)
                            act.activation(ex[:, h, 0, :], low[:, h, 0, :], ACT.Exp).then_inc(sm["ex"], 1)
                        for h in range(2):
                            act.wait_ge(sm["ex"], i * 2 + h + 1)
                            act.activation(low[:, h, 0, :], ex[:, h, 0, :], ACT.Ln, bias=1.0).then_inc(sm["ln"], 1)
                        for h in range(2):
                            act.wait_ge(sm["xTps"], i * 2 + h + 1)
                            act.wait_ge(sm["stored"], block_done(i * 2 + h - 2))
                            act.copy(xT[:, h, :], one_ps[h][:, :]).then_inc(sm["xT"], 1)
                        for h in range(2):
                            act.wait_ge(sm["low2"], i * 2 + h + 1)
                            act.activation(ex[:, h, :, :], low[:, h, :, :], ACT.Exp).then_inc(sm["ex2"], 1)
                        for h in range(2):
                            act.wait_ge(sm["ex2"], i * 2 + h + 1)
                            act.activation(low[:, h, :, :], ex[:, h, :, :], ACT.Ln, bias=1.0).then_inc(sm["ln2"], 1)

                @block.tensor
                def _(pe):
                    pe.wait_ge(w_in, 48)
                    with pe.Fori(0, PAIRS) as i:
                        for h in range(2):
                            pe.wait_ge(sm["xp"], i * 2 + h + 1)
                            pe.wait_ge(sm["vu"], block_done(i * 2 + h - 2))
                            for j in range(4):
                                col = slice(j * P, (j + 1) * P)
                                m = pe.transpose(one_ps[h][:, col], xp[:, h, col], ident[:, :])
                            m.then_inc(sm["xTps"], 1)
                        for h in range(2):
                            pe.wait_ge(sm["xT"], i * 2 + h + 1)
                            for j in range(4):
                                col = slice(j * P, (j + 1) * P)
                                pe.matmul(two_ps[h][:, col], ones_row[:, :], bj_row[:, :], start=True, stop=False)
                                pe.matmul(two_ps[h][:, col], xT[:, h, col], wts[:, WJ, :], start=False, stop=True)
                            pe.matmul(one_ps[h][:, :], wts[:, WI, :], xT[:, h, :], start=True, stop=True
                                      ).then_inc(sm["vups"], 1)
            end_stage()

        with ExitStack() as s:
            stage.append(s)
            b = scatter_buffers("pair", True)
            windowed = scatter_pass(b, v_tab, dst_f, 0, src_f, pair_acc, True, True)
            gathered = scatter_pass(b, v_tab, dst_f, 0, src_f, pair_acc, True, False)
            with nc.Block() as block:
                @block.sync
                def _(sp):
                    with sp.If(fits_here(sp)):
                        windowed[0](sp)
                    with sp.Else():
                        gathered[0](sp)

                @block.gpsimd
                def _(pool):
                    with pool.If(fits_here(pool)):
                        windowed[1](pool)
                    with pool.Else():
                        gathered[1](pool)

                @block.tensor
                def _(pe):
                    with pe.If(fits_here(pe)):
                        windowed[2](pe)
                    with pe.Else():
                        gathered[2](pe)

                @block.vector
                def _(dve):
                    with dve.If(fits_here(dve)):
                        windowed[3](dve)
                    with dve.Else():
                        gathered[3](dve)

                @block.scalar
                def _(act):
                    with act.If(fits_here(act)):
                        windowed[4](act)
                    with act.Else():
                        gathered[4](act)
            end_stage()

        with ExitStack() as s:
            stage.append(s)
            wts = sb("n2wts", [P, 9, P])
            cols = sb("n2cols", [P, 9])
            parts = sb("n2parts", [P, 2, ACCS, NB])
            x1 = sb("n2x1", [P, 2, NB])
            xT = sb("n2xT", [P, 2, NB])
            u0 = sb("n2u0", [P, 2, NB])
            u = sb("n2u", [P, 2, NB])
            low = sb("n2low", [P, 2, NB])
            ex = sb("n2ex", [P, 2, NB])
            sp_u = sb("n2sp", [P, 2, NB])
            gx = sb("n2gx", [P, 2, NB])
            res = sb("n2res", [P, 2, NB])
            stats = sb("n2stats", [P, 2, 4, 6])
            mv = sb("n2mv", [P, 2, 4, 2])
            var = sb("n2var", [P, 2, 4])
            rstd = sb("n2rstd", [P, 2, 4])
            half4 = sb("n2half", [P, 4])
            one_ps = [ps(f"n2one{h}", [P, NB]) for h in range(2)]
            two_ps = [ps(f"n2two{h}", [P, NB]) for h in range(2)]
            names = ("summed", "low", "ex", "ln", "sp", "mm", "u", "gx", "o", "oT", "joined", "stats", "mv", "var",
                     "rstd", "res", "stored")
            sm2 = {k: sem("n2_" + k) for k in names}
            w_in = sem("n2_w_in")
            sync_passed = sem("n2_sync_passed")
            half_made = sem("n2_half_made")
            loaded = [sem(f"n2_loaded{h}") for h in range(2)]
            stores = [sem(f"n2_stores{h}") for h in range(2)]
            LOADS = (ACCS + 3) * 16
            SOFTS = 7
            MMS = 7

            def block_done(n):
                return n + 3

            def nth(i, many, k, h):
                return i * (2 * many) + (2 * k + h + 1)

            with nc.Block() as block:
                @block.sync
                def _(sp):
                    sp.dma_start(wts[:, :, :], ins["WT"]).then_inc(w_in, 16)
                    sp.dma_start(cols[:, :], ins["cols"]).then_inc(w_in, 16)

                    def load(i, h):
                        at = bass.ds(i * (2 * NB) + h * NB, NB)
                        for q in range(ACCS):
                            sp.dma_start(parts[:, h, q, :].rearrange("p (j f) -> p j f", f=P),
                                         pair_acc[q][at, :].rearrange("(j p) f -> p j f", p=P)).then_inc(loaded[h], 16)
                        sp.dma_start(x1[:, h, :].rearrange("p (j f) -> p j f", f=P),
                                     x1_tab[at, :].rearrange("(j p) f -> p j f", p=P)).then_inc(loaded[h], 16)
                        sp.dma_start(xT[:, h, :], xT_tab[:, at]).then_inc(loaded[h], 16)
                        sp.dma_start(u0[:, h, :], uT_tab[:, at]).then_inc(loaded[h], 16)

                    def pair(i, last):
                        for h in range(2):
                            at = bass.ds(i * (2 * NB) + h * NB, NB)
                            sp.wait_ge(sm2["joined"], i * 2 + h + 1)
                            sp.sem_inc(sync_passed, 1)
                            if not last:
                                load(i + 1, h)
                            sp.wait_ge(sm2["res"], block_done(i * 2 + h))
                            sp.sem_inc(sync_passed, 1)
                            sp.dma_start(out[at, :].rearrange("(j p) f -> p j f", p=P),
                                         res[:, h, :].rearrange("p (j f) -> p j f", f=P)).then_inc(stores[h], 16)
                        for h in range(2):
                            sp.wait_ge(stores[h], i * 16 + 16)
                            sp.sem_inc(sm2["stored"], 1)

                    sp.sem_inc(sm2["stored"], 2)
                    load(0, 0)
                    load(0, 1)
                    if PAIRS > 1:
                        with sp.Fori(0, PAIRS - 1) as i:
                            pair(i, False)
                    pair(PAIRS - 1, True)

                @block.gpsimd
                def _(pool):
                    pool.memset(half4[:, :], -0.5).then_inc(half_made, 1)
                    pool.wait_ge(half_made, 1)
                    with pool.Fori(0, PAIRS) as i:
                        for h in range(2):
                            pool.wait_ge(sm2["var"], i * 2 + h + 1)
                            pool.tensor_tensor(rstd[:, h, :], var[:, h, :], half4[:, :], ALU.pow).then_inc(sm2["rstd"], 1)

                @block.vector
                def _(dve):
                    dve.wait_ge(w_in, 32)
                    dve.sem_inc(sm2["res"], 2)
                    with dve.Fori(0, PAIRS) as i:
                        for h in range(2):
                            dve.wait_ge(loaded[h], i * LOADS + LOADS)
                            dve.wait_ge(sm2["summed"], i * 2 + h + 1)
                            dve.wait_ge(sm2["res"], block_done(i * 2 + h - 2))
                            dve.tensor_tensor(u[:, h, :], u0[:, h, :], one_ps[h][:, :], ALU.add
                                              ).then_inc(sm2["u"], 1)
                            dve.tensor_scalar(gx[:, h, :], xT[:, h, :], cols[:, GATE:GATE + 1], cols[:, BV:BV + 1],
                                              ALU.mult, ALU.add).then_inc(sm2["gx"], 1)
                        for k in range(SOFTS):
                            layer = k // 2
                            inner = k % 2 == 1
                            bias = cols[:, B1 + layer:B1 + layer + 1] if inner else None
                            for h in range(2):
                                if inner:
                                    dve.wait_ge(sm2["mm"], nth(i, MMS, 2 * layer, h))
                                    dve.tensor_scalar(low[:, h, :], one_ps[h][:, :], bias, CAP, ALU.add, ALU.min
                                                      ).then_inc(sm2["low"], 1)
                                else:
                                    dve.wait_ge(sm2["u"], nth(i, 4, layer, h))
                                    dve.tensor_scalar(low[:, h, :], u[:, h, :], CAP, None, ALU.min
                                                      ).then_inc(sm2["low"], 1)
                            for h in range(2):
                                dve.wait_ge(sm2["ln"], nth(i, SOFTS, k, h))
                                if inner:
                                    dve.scalar_tensor_tensor(out=sp_u[:, h, :], in0=one_ps[h][:, :], scalar=bias,
                                                             in1=low[:, h, :], op0=ALU.add, op1=ALU.max
                                                             ).then_inc(sm2["sp"], 1)
                                else:
                                    dve.tensor_tensor(sp_u[:, h, :], u[:, h, :], low[:, h, :], ALU.max
                                                      ).then_inc(sm2["sp"], 1)
                            if inner:
                                for h in range(2):
                                    dve.wait_ge(sm2["mm"], nth(i, MMS, 2 * layer + 1, h))
                                    dve.scalar_tensor_tensor(out=u[:, h, :], in0=two_ps[h][:, :],
                                                             scalar=cols[:, B2 + layer:B2 + layer + 1],
                                                             in1=u[:, h, :], op0=ALU.add, op1=ALU.add
                                                             ).then_inc(sm2["u"], 1)
                        for h in range(2):
                            dve.wait_ge(sm2["mm"], nth(i, MMS, 6, h))
                            dve.wait_ge(sm2["gx"], i * 2 + h + 1)
                            dve.tensor_tensor(gx[:, h, :], one_ps[h][:, :], gx[:, h, :], ALU.add).then_inc(sm2["o"], 1)
                        for h in range(2):
                            dve.wait_ge(sm2["oT"], i * 2 + h + 1)
                            dve.tensor_tensor(u[:, h, :], two_ps[h][:, :], x1[:, h, :], ALU.add
                                              ).then_inc(sm2["joined"], 1)
                        for h in range(2):
                            dve.wait_ge(sm2["joined"], i * 2 + h + 1)
                            for j in range(4):
                                m = dve.bn_stats(stats[:, h, j, :], u[:, h, j * P:(j + 1) * P])
                            m.then_inc(sm2["stats"], 1)
                        for h in range(2):
                            dve.wait_ge(sm2["stats"], 1)
                            dve.wait_ge(sm2["stats"], i * 2 + h + 1)
                            for j in range(4):
                                m = dve.bn_aggr(mv[:, h, j, :], stats[:, h, j, :])
                            m.then_inc(sm2["mv"], 1)
                        for h in range(2):
                            dve.wait_ge(sm2["mv"], i * 2 + h + 1)
                            dve.tensor_scalar(var[:, h, :], mv[:, h, :, 1], EPS, None, ALU.add).then_inc(sm2["var"], 1)
                        for h in range(2):
                            dve.wait_ge(sm2["rstd"], i * 2 + h + 1)
                            dve.wait_ge(sm2["stored"], block_done(i * 2 + h - 2))
                            for j in range(4):
                                col = slice(j * P, (j + 1) * P)
                                m = dve.tensor_scalar(res[:, h, col], u[:, h, col], mv[:, h, j, 0:1],
                                                      rstd[:, h, j:j + 1], ALU.subtract, ALU.mult)
                            m.then_inc(sm2["res"], 1)

                @block.scalar
                def _(act):
                    with act.Fori(0, PAIRS) as i:
                        for k in range(SOFTS):
                            for h in range(2):
                                act.wait_ge(sm2["low"], nth(i, SOFTS, k, h))
                                act.activation(ex[:, h, :], low[:, h, :], ACT.Exp).then_inc(sm2["ex"], 1)
                            for h in range(2):
                                act.wait_ge(sm2["ex"], nth(i, SOFTS, k, h))
                                act.activation(low[:, h, :], ex[:, h, :], ACT.Ln, bias=1.0).then_inc(sm2["ln"], 1)

                @block.tensor
                def _(pe):
                    pe.wait_ge(w_in, 32)
                    pe.sem_inc(sm2["o"], 2)
                    with pe.Fori(0, PAIRS) as i:
                        for h in range(2):
                            pe.wait_ge(loaded[h], i * LOADS + LOADS)
                            pe.wait_ge(sm2["o"], block_done(i * 2 + h - 2))
                            for j in range(4):
                                col = slice(j * P, (j + 1) * P)
                                for q in range(ACCS):
                                    m = pe.matmul(one_ps[h][:, col], parts[:, h, q, col], ident[:, :], start=q == 0,
                                                  stop=q == ACCS - 1)
                            m.then_inc(sm2["summed"], 1)
                        for k in range(SOFTS):
                            layer = k // 2
                            w = WV if k == 6 else (W2 if k % 2 else W1) + layer
                            to = two_ps if k % 2 else one_ps
                            for h in range(2):
                                pe.wait_ge(sm2["sp"], nth(i, SOFTS, k, h))
                                pe.matmul(to[h][:, :], wts[:, w, :], sp_u[:, h, :], start=True, stop=True
                                          ).then_inc(sm2["mm"], 1)
                        for h in range(2):
                            pe.wait_ge(sm2["o"], block_done(i * 2 + h))
                            for j in range(4):
                                col = slice(j * P, (j + 1) * P)
                                m = pe.transpose(two_ps[h][:, col], gx[:, h, col], ident[:, :])
                            m.then_inc(sm2["oT"], 1)
            end_stage()


def kernel(x, src, dst, edge_attr_64, edge_weight, L1_gnn_Wg, L1_gnn_Wi, L1_gnn_bi, L1_gnn_Wj, L1_gnn_bj,
           L1_gnn_Wv, L1_gnn_bv, L1_gnn_gate, L1_gnn_res_W1, L1_gnn_res_b1, L1_gnn_res_W2, L1_gnn_res_b2):
    import numpy as np
    import concourse.bacc as bacc
    from concourse.bass_utils import run_bass_kernel_spmd

    n, edges = x.shape[0], src.shape[0]
    chunks, nrows = sizes(n, edges)
    tiles = chunks * CT
    epad = tiles * P - edges

    src = np.concatenate([np.asarray(src), np.full(epad, n, src.dtype)])
    dst = np.concatenate([np.asarray(dst), np.full(epad, n, dst.dtype)])
    attr = np.concatenate([np.asarray(edge_attr_64), np.zeros((epad, R), np.float32)])
    weights = np.concatenate([np.asarray(L1_gnn_Wi)[None], np.asarray(L1_gnn_Wj)[None], np.asarray(L1_gnn_res_W1),
                              np.asarray(L1_gnn_res_W2), np.asarray(L1_gnn_Wv)[None]])
    cols = np.concatenate([np.asarray(L1_gnn_bi)[None], np.asarray(L1_gnn_res_b1), np.asarray(L1_gnn_res_b2),
                           np.asarray(L1_gnn_bv)[None], np.asarray(L1_gnn_gate)[None]])
    arrays = {
        "x": np.concatenate([np.asarray(x), np.zeros((nrows - n, P), np.float32)]),
        "src_col": src.reshape(tiles, P).T, "dst_col": dst.reshape(tiles, P).T,
        "src_row": src.reshape(P, tiles), "dst_row": dst.reshape(P, tiles),
        "attr_t": attr.T,
        "WgT": np.asarray(L1_gnn_Wg).T,
        "WT": weights.transpose(2, 0, 1),
        "cols": cols.T,
        "bj": np.asarray(L1_gnn_bj)[None],
    }
    arrays = {f"in_{k}": np.ascontiguousarray(a) for k, a in arrays.items()}
    nc = bacc.Bacc("TRN2", target_bir_lowering=False, num_devices=1)
    ins = {k[3:]: nc.dram_tensor(k, a.shape, mybir.dt.from_np(a.dtype), kind="ExternalInput").ap()
           for k, a in arrays.items()}
    out = nc.dram_tensor("out_0", [nrows, P], F32, kind="ExternalOutput").ap()
    gnn_kernel(nc, n, ins, out)
    r = run_bass_kernel_spmd(nc, [arrays], core_ids=[0])
    return r.results[0]["out_0"][:n]
```

```python
from contextlib import ExitStack

import concourse.bass as bass
from concourse import mybir

P = 128
GT = 4
CG = 6
CT = GT * CG
GE = GT * P
CE = CT * P
ACCS = 6
NB = 512
LAG = 3
STREAMS = 5
R = 64

F32 = mybir.dt.float32
BF16 = mybir.dt.bfloat16
I32 = mybir.dt.int32
ALU = mybir.AluOpType
ACT = mybir.ActivationFunctionType


def sizes(n_nodes, n_edges):
    chunks = -(-n_edges // CE)
    blocks = STREAMS * -(-(n_nodes + 1 + 2 * P) // (STREAMS * NB))
    return chunks, blocks * NB


def gnn_kernel(nc, n_edges, ins, out):
    T = ins["src_col"].shape[1]
    CH = T // CT
    LG = max(LAG, -(-(n_edges - (CH - 1) * CE) // GE))
    NROWS = ins["x"].shape[0]
    NT = NROWS // P
    BLOCKS = NROWS // NB
    SPARE = NROWS - P
    EPAD = T * P
    HIS = NT
    SHIFT = 3
    WLO = 1 << SHIFT
    WHI = P // WLO
    MT = 2
    RING = 6
    ZEROS = NROWS // 8

    ctx = ExitStack()
    with ctx:
        def dram(name, shape, dt):
            return nc.dram_tensor(name, shape, dt, kind="Internal").ap()

        y_tab = dram("y_tab", [NROWS, P], F32)
        v_tab = dram("v_tab", [NROWS, P], F32)
        x1_tab = dram("x1_tab", [NROWS, P], F32)
        xT_tab = dram("xT_tab", [P, NROWS], F32)
        uT_tab = dram("uT_tab", [P, NROWS], F32)
        rows_tab = dram("rows_tab", [2, 2, EPAD], BF16)
        conv_acc = [dram(f"conv_acc{q}", [NROWS, P], F32) for q in range(ACCS)]
        pair_acc = [dram(f"pair_acc{q}", [NROWS, P], F32) for q in range(ACCS)]

        stage = [ctx]
        held = []

        def clear(eng, acc, to):
            eng.dma_start(acc.rearrange("(p a) f -> p (a f)", p=P),
                          zeros[:, :].unsqueeze(1).to_broadcast([P, NROWS // ZEROS, ZEROS])).then_inc(to, 16)

        def sb(name, shape, dt=F32):
            return stage[-1].enter_context(nc.sbuf_tensor(name, shape, dt))

        def ps(name, shape, dt=F32):
            return stage[-1].enter_context(nc.psum_tensor(name, shape, dt))

        def sem(name):
            held.append(nc.alloc_semaphore(name))
            return held[-1]

        def end_stage():
            stage.pop()
            nc.clear_and_free_semaphores(held[:])
            nc.all_engine_barrier()
            held.clear()

        ident = sb("ident", [P, P])
        not_earlier = sb("not_earlier", [P, P])
        spare_row = sb("spare_row", [P, 1])
        hilo_w = sb("hilo_w", [2, P], BF16)
        dis = sb("dis", [P, NT])
        iota = sb("iota", [P, P])
        iota_b = sb("iota_b", [P, P], BF16)
        base_p = sb("base_p", [P, CH])
        base_i = sb("base_i", [1, CH], I32)
        window_block = sb("window_block", [1, CH], I32)
        window_place = sb("window_place", [P, CH, 3])
        fits = sb("fits", [1, 1], I32)
        zeros = sb("zeros", [P, ZEROS])
        deg = sb("deg", [P, NT])

        edge_scope = ctx.enter_context(ExitStack())
        stage.append(edge_scope)
        src_f = sb("src_f", [P, T])
        dst_f = sb("dst_f", [P, T])
        in_window = sb("in_window", [P, T])
        stage.pop()

        def fits_here(eng):
            return eng.value_load(fits[0:1, 0:1], min_val=0, max_val=P) == P

        with ExitStack() as s:
            stage.append(s)
            src_i = sb("src_i", [P, T], I32)
            dst_i = sb("dst_i", [P, T], I32)
            rows_i = sb("rows_i", [P, 2, T], I32)
            part_i = sb("part_i", [P, T], I32)
            rows_b = sb("rows_b", [P, 2, 2, T], BF16)
            iota_i = sb("iota_i", [P, P], I32)
            row_i = sb("row_i", [P, 1], I32)
            hi_w = sb("hi_w", [2, 1])
            first_p = sb("first_p", [P, P])
            part_p = sb("part_p", [P, 1])
            base = sb("base", [P, CH])
            reach = sb("reach", [P, 2])
            within = sb("within", [P, 2])
            both = sb("both", [P, 1])
            ones_col = sb("ones_col", [P, 1])
            base_ps = ps("base_ps", [P, CH])
            fits_ps = ps("fits_ps", [P, 1])
            dst_in, src_in, rows_in, rows_out = sem("dst_in"), sem("src_in"), sem("rows_in"), sem("rows_out")
            iota_made, consts, pool_own, masks = sem("iota_made"), sem("consts"), sem("pool_own"), sem("masks")
            cast, based, compared, fitted = sem("cast"), sem("based"), sem("compared"), sem("fitted")
            dve_own, parts_made, rows_made, zeroed = sem("dve_own"), sem("parts_made"), sem("rows_made"), sem("zeroed")
            acc_cleared = sem("acc_cleared")

            with nc.Block() as block:
                @block.sync
                def _(sp):
                    sp.dma_start(dst_i[:, :], ins["dst_col"]).then_inc(dst_in, 16)
                    sp.dma_start(src_i[:, :], ins["src_col"]).then_inc(src_in, 16)
                    sp.dma_start(rows_i[:, 0, :], ins["src_row"]).then_inc(rows_in, 16)
                    sp.dma_start(rows_i[:, 1, :], ins["dst_row"]).then_inc(rows_in, 16)
                    sp.wait_ge(zeroed, 1)
                    clear(sp, conv_acc[0], acc_cleared)
                    for q in range(ACCS):
                        clear(sp, pair_acc[q], acc_cleared)
                    sp.wait_ge(rows_made, 4)
                    for k in range(2):
                        for s_ in range(2):
                            sp.dma_start(rows_tab[k, s_, :].rearrange("(p t) -> p t", t=T),
                                         rows_b[:, k, s_, :]).then_inc(rows_out, 16)

                @block.gpsimd
                def _(pool):
                    pool.iota(iota_i[:, :], [[1, P]], base=0, channel_multiplier=0).then_inc(iota_made, 1)
                    pool.iota(row_i[:, :], [[0, 1]], base=SPARE, channel_multiplier=1).then_inc(iota_made, 1)
                    pool.memset(ident[:, :], 0.0).then_inc(pool_own, 1)
                    pool.memset(not_earlier[:, :], 1.0).then_inc(pool_own, 1)
                    pool.memset(hi_w[:, :], 1.0).then_inc(pool_own, 1)
                    pool.wait_ge(pool_own, 3)
                    pool.affine_select(out=ident[:, :], in_=ident[:, :], compare_op=ALU.not_equal, fill=1.0,
                                       base=0, pattern=[[-1, P]], channel_multiplier=1).then_inc(masks, 1)
                    pool.affine_select(out=not_earlier[:, :], in_=not_earlier[:, :], compare_op=ALU.is_ge,
                                       fill=0.0, base=0, pattern=[[-1, P]], channel_multiplier=1).then_inc(masks, 1)
                    pool.affine_select(out=hi_w[:, :], in_=hi_w[:, :], compare_op=ALU.not_equal, fill=128.0,
                                       base=0, pattern=[[0, 1]], channel_multiplier=1).then_inc(masks, 1)

                @block.vector
                def _(dve):
                    dve.memset(zeros[:, :], 0.0).then_inc(zeroed, 1)
                    dve.memset(ones_col[:, :], 1.0)
                    dve.memset(hilo_w[:, :], 1.0)
                    dve.memset(first_p[:, :], 0.0).then_inc(consts, 1)
                    dve.wait_ge(consts, 1)
                    dve.memset(first_p[0:1, :], 1.0)
                    dve.wait_ge(iota_made, 2)
                    dve.tensor_copy(iota[:, :], iota_i[:, :])
                    dve.tensor_copy(iota_b[:, :], iota_i[:, :])
                    dve.tensor_copy(spare_row[:, :], row_i[:, :]).then_inc(consts, 1)
                    dve.wait_ge(consts, 2)
                    dve.tensor_scalar(part_p[:, :], spare_row[:, :], -float(SPARE), None, ALU.add)
                    dve.wait_ge(masks, 3)
                    dve.tensor_scalar(hilo_w[:, :], hilo_w[:, :], hi_w[:, 0:1], None, ALU.mult)
                    dve.wait_ge(dst_in, 16)
                    dve.tensor_copy(dst_f[:, :], dst_i[:, :]).then_inc(cast, 1)
                    dve.wait_ge(src_in, 16)
                    dve.tensor_copy(src_f[:, :], src_i[:, :]).then_inc(cast, 1)

                    dve.wait_ge(based, 1)
                    dve.tensor_copy(base[:, :], base_ps[:, :]).then_inc(dve_own, 1)
                    dve.wait_ge(dve_own, 1)
                    dve.tensor_copy(base_i[:, :], base[0:1, :])
                    dve.tensor_scalar(base_p[:, :], base[:, :], part_p[:, 0:1], None, ALU.add)
                    dve.tensor_tensor(in_window[:, :].rearrange("p (c t) -> p c t", t=CT),
                                      dst_f[:, :].rearrange("p (c t) -> p c t", t=CT),
                                      base[:, :].unsqueeze(2).to_broadcast([P, CH, CT]), ALU.subtract
                                      ).then_inc(dve_own, 1)
                    dve.wait_ge(dve_own, 2)
                    dve.tensor_reduce(reach[:, 0:1], in_window[:, :], mybir.AxisListType.X, ALU.min)
                    dve.tensor_reduce(reach[:, 1:2], in_window[:, :], mybir.AxisListType.X, ALU.max
                                      ).then_inc(dve_own, 1)
                    dve.wait_ge(dve_own, 3)
                    dve.tensor_scalar(within[:, 0:1], reach[:, 0:1], 0.0, None, ALU.is_ge)
                    dve.tensor_scalar(within[:, 1:2], reach[:, 1:2], float(P), None, ALU.is_lt).then_inc(dve_own, 1)
                    dve.wait_ge(dve_own, 4)
                    dve.tensor_tensor(both[:, :], within[:, 0:1], within[:, 1:2], ALU.mult).then_inc(compared, 1)
                    dve.wait_ge(fitted, 1)
                    dve.tensor_copy(fits[:, :], fits_ps[0:1, :])

                    dve.wait_ge(cast, 2)
                    dve.wait_ge(rows_in, 32)
                    for n, (s_, k) in enumerate(((0, 0), (0, 1), (1, 0), (1, 1))):
                        part = (part_i, src_i)[n % 2]
                        if n >= 2:
                            dve.wait_ge(rows_made, n - 1)
                        if k == 0:
                            dve.tensor_scalar(part[:, :], rows_i[:, s_, :], 7, None, ALU.arith_shift_right
                                              ).then_inc(parts_made, 1)
                        else:
                            dve.tensor_scalar(part[:, :], rows_i[:, s_, :], 127, None, ALU.bitwise_and
                                              ).then_inc(parts_made, 1)

                @block.scalar
                def _(act):
                    for n, (s_, k) in enumerate(((0, 0), (0, 1), (1, 0), (1, 1))):
                        act.wait_ge(parts_made, n + 1)
                        act.copy(rows_b[:, k, s_, :], (part_i, src_i)[n % 2][:, :]).then_inc(rows_made, 1)

                @block.tensor
                def _(pe):
                    pe.wait_ge(cast, 1)
                    pe.matmul(base_ps[:, :], first_p[:, :],
                              dst_f[:, :].rearrange("p (c t) -> p c t", t=CT)[:, :, 0], start=True, stop=True
                              ).then_inc(based, 1)
                    pe.wait_ge(compared, 1)
                    pe.matmul(fits_ps[0:1, :], both[:, :], ones_col[:, :], start=True, stop=True).then_inc(fitted, 1)

            hi_hot = sb("hi_hot", [P, 2, 8, HIS], BF16)
            lo_hot = sb("lo_hot", [P, 2, 8, P], BF16)
            high = sb("high", [P, T], BF16)
            low = sb("low", [P, T], BF16)
            ramp_i = sb("ramp_i", [P, CT // MT, WHI, MT], I32)
            ramp = sb("ramp", [P, CT // MT, WHI, MT], BF16)
            high_hot = sb("high_hot", [P, 2, CT // MT, WHI, MT], BF16)
            low_hot = sb("low_hot", [P, 2, CT // MT, WLO, MT], BF16)
            spread = sb("spread", [MT * WHI, MT * WLO, P])
            parts = sb("parts", [MT * WHI, CH, MT * WLO])
            node_i = sb("node_i", [P, 3, CH], I32)
            base_blocks = sb("base_blocks", [P, 2, CH], I32)
            base_hi = sb("base_hi", [P, CH])
            node_hi = sb("node_hi", [P, CH])
            node_lo = sb("node_lo", [P, CH])
            count = sb("count", [P, CH])
            whi_hot = sb("whi_hot", [P, RING, HIS])
            wlo_hot = sb("wlo_hot", [P, RING, P])
            deg_ps = ps("deg_ps", [P, HIS])
            parts_ps = ps("parts_ps", [MT * WHI, -(-CH * MT * WLO // NB) * NB])
            count_ps = base_ps
            blocks_made = sem("blocks_made")
            hots, hots_used, columns, split = sem("hots"), sem("hots_used"), sem("columns"), sem("split")
            counted, whots, whots_used, summed = sem("wcounted"), sem("whots"), sem("whots_used"), sem("deg_summed")
            spread_own, spread_made, ramp_made = sem("spread_own"), sem("spread_made"), sem("ramp_made")
            NG = T // 8

            with nc.Block() as block:
                @block.sync
                def _(sp):
                    sp.wait_ge(rows_out, 64)
                    sp.wait_ge(acc_cleared, 16 * (ACCS + 1))

                @block.gpsimd
                def _(pool):
                    pool.iota(ramp_i[:, :, :, :], [[0, CT // MT], [1, WHI], [0, MT]], base=0, channel_multiplier=0).then_inc(ramp_made, 1)
                    pool.memset(spread[:, :, :], 0.0).then_inc(spread_own, 1)
                    pool.wait_ge(spread_own, 1)
                    for t in range(MT):
                        layers = spread[:, t::MT, :].rearrange("q b (a l) -> q b a l", l=WLO)
                        pool.affine_select(out=layers, in_=layers, compare_op=ALU.not_equal, fill=1.0, base=-t,
                                           pattern=[[-P, WLO], [-MT, WHI], [P, WLO]], channel_multiplier=1
                                           ).then_inc(spread_made, 1)

                @block.vector
                def _(dve):
                    with dve.If(fits_here(dve)):
                        dve.tensor_copy(dst_i[:, :], in_window[:, :]).then_inc(split, 1)
                        dve.wait_ge(split, 1)
                        dve.tensor_scalar(part_i[:, :], dst_i[:, :], SHIFT, None, ALU.arith_shift_right)
                        dve.tensor_scalar(src_i[:, :], dst_i[:, :], WLO - 1, None, ALU.bitwise_and
                                          ).then_inc(split, 1)
                        dve.wait_ge(split, 2)
                        dve.tensor_copy(high[:, :], part_i[:, :])
                        dve.tensor_copy(low[:, :], src_i[:, :])
                        dve.wait_ge(ramp_made, 1)
                        dve.tensor_copy(ramp[:, :, :, :], ramp_i[:, :, :, :]).then_inc(split, 1)
                        dve.wait_ge(split, 3)

                        def place_hots(c, par):
                            dve.wait_ge(hots_used, c + 1)
                            for hot, part, width in ((high_hot, high, WHI), (low_hot, low, WLO)):
                                m = dve.tensor_tensor(
                                    hot[:, par, :, :, :], ramp[:, :, 0:width, :],
                                    part[:, bass.ds(c * CT, CT)].rearrange("p (n t) -> p n t", t=MT).unsqueeze(2
                                    ).to_broadcast([P, CT // MT, width, MT]),
                                    ALU.is_equal)
                            m.then_inc(hots, 1)

                        with dve.Fori(0, CH // 2) as i:
                            for par in range(2):
                                place_hots(i * 2 + par, par)
                        if CH % 2:
                            place_hots(CH - 1, 0)
                        dve.tensor_copy(base_blocks[:, 0, :], base[:, :])
                        dve.tensor_copy(node_i[:, 0, :], base_p[:, :]).then_inc(split, 1)
                        dve.wait_ge(split, 4)
                        dve.tensor_scalar(base_blocks[:, 1, :], base_blocks[:, 0, :], 7, None, ALU.arith_shift_right)
                        dve.tensor_scalar(node_i[:, 1, :], node_i[:, 0, :], 7, None, ALU.arith_shift_right)
                        dve.tensor_scalar(node_i[:, 2, :], node_i[:, 0, :], 127, None, ALU.bitwise_and
                                          ).then_inc(split, 1)
                        dve.wait_ge(split, 5)
                        dve.tensor_copy(node_hi[:, :], node_i[:, 1, :])
                        dve.tensor_copy(node_lo[:, :], node_i[:, 2, :])
                        dve.tensor_copy(base_hi[:, :], base_blocks[:, 1, :])
                        dve.tensor_copy(window_block[:, :], base_blocks[0:1, 1, :]).then_inc(blocks_made, 1)
                        dve.wait_ge(blocks_made, 1)
                        dve.tensor_copy(window_place[:, :, 0], node_lo[:, :])
                        dve.tensor_tensor(window_place[:, :, 1], node_hi[:, :], base_hi[:, :], ALU.is_equal)
                        dve.tensor_tensor(window_place[:, :, 2], node_hi[:, :], base_hi[:, :], ALU.is_gt)
                        dve.wait_ge(counted, 1)
                        dve.tensor_copy(parts[:, :, :].rearrange("a c b -> a (c b)"), parts_ps[:, 0:CH * MT * WLO]
                                        ).then_inc(counted, 1)
                        dve.wait_ge(counted, 3)
                        dve.tensor_copy(count[:, :], count_ps[:, :]).then_inc(split, 1)
                        dve.wait_ge(split, 6)
                        for c in range(CH):
                            if c >= RING:
                                dve.wait_ge(whots_used, c + 1 - RING)
                            dve.tensor_scalar(wlo_hot[:, c % RING, :], iota[:, :], node_lo[:, c:c + 1], None,
                                              ALU.is_equal)
                            dve.tensor_scalar(whi_hot[:, c % RING, :], iota[:, 0:HIS], node_hi[:, c:c + 1],
                                              count[:, c:c + 1], ALU.is_equal, ALU.mult).then_inc(whots, 1)
                    with dve.Else():
                        dve.tensor_scalar(part_i[:, :], dst_i[:, :], 7, None, ALU.arith_shift_right
                                          ).then_inc(split, 1)
                        dve.wait_ge(split, 1)
                        dve.tensor_copy(high[:, :], part_i[:, :]).then_inc(split, 1)
                        dve.wait_ge(split, 2)
                        dve.tensor_scalar(part_i[:, :], dst_i[:, :], 127, None, ALU.bitwise_and).then_inc(split, 1)
                        dve.wait_ge(split, 3)
                        dve.tensor_copy(low[:, :], part_i[:, :]).then_inc(split, 1)
                        dve.wait_ge(split, 4)

                        def one_hots(par, t):
                            dve.tensor_tensor(lo_hot[:, par, :, :],
                                              iota_b[:, :].unsqueeze(1).to_broadcast([P, 8, P]),
                                              low[:, bass.ds(t, 8)].unsqueeze(2).to_broadcast([P, 8, P]),
                                              ALU.is_equal)
                            dve.tensor_tensor(hi_hot[:, par, :, :],
                                              iota_b[:, 0:HIS].unsqueeze(1).to_broadcast([P, 8, HIS]),
                                              high[:, bass.ds(t, 8)].unsqueeze(2).to_broadcast([P, 8, HIS]),
                                              ALU.is_equal).then_inc(hots, 1)

                        with dve.Fori(0, NG // 2) as i:
                            for par in range(2):
                                dve.wait_ge(hots_used, i * 2 + (par + 1))
                                one_hots(par, i * 16 + par * 8)
                        if NG % 2:
                            dve.wait_ge(hots_used, NG)
                            one_hots(0, (NG - 1) * 8)

                    dve.wait_ge(summed, 1)
                    dve.tensor_copy(deg[:, :], deg_ps[:, 0:NT])

                @block.tensor
                def _(pe):
                    with pe.If(fits_here(pe)):
                        pe.sem_inc(hots_used, 2)

                        def count_places(c, par):
                            pe.wait_ge(hots, c + 1)
                            for n in range(CT // MT):
                                m = pe.matmul(parts_ps[:, bass.ds(c * (MT * WLO), MT * WLO)],
                                              high_hot[:, par, n, :, :].rearrange("p a t -> p (a t)"),
                                              low_hot[:, par, n, :, :].rearrange("p b t -> p (b t)"),
                                              start=n == 0, stop=n == CT // MT - 1)
                            m.then_inc(hots_used, 1)

                        with pe.Fori(0, CH // 2) as i:
                            for par in range(2):
                                count_places(i * 2 + par, par)
                        if CH % 2:
                            count_places(CH - 1, 0)
                        pe.wait_ge(hots_used, 2 + CH)
                        pe.sem_inc(counted, 1)
                        pe.wait_ge(spread_made, MT)
                        pe.wait_ge(counted, 2)
                        for b in range(MT * WLO):
                            m = pe.matmul(count_ps[:, :], spread[:, b, :], parts[:, :, b], start=b == 0,
                                          stop=b == MT * WLO - 1)
                        m.then_inc(counted, 1)
                        for c in range(CH):
                            pe.wait_ge(whots, c + 1)
                            m = pe.matmul(deg_ps[:, :], wlo_hot[:, c % RING, :], whi_hot[:, c % RING, :],
                                          start=c == 0, stop=c == CH - 1)
                            m.then_inc(whots_used if c < CH - 1 else summed, 1)
                    with pe.Else():
                        pe.sem_inc(hots_used, 2)
                        pe.matmul(deg_ps[:, :], zeros[:, 0:P], zeros[:, 0:HIS], start=True, stop=False)

                        def products(par):
                            for k in range(8):
                                m = pe.matmul(deg_ps[:, :], lo_hot[:, par, k, :], hi_hot[:, par, k, :],
                                              start=False, stop=False)
                            m.then_inc(hots_used, 1)

                        with pe.Fori(0, NG // 2) as i:
                            for par in range(2):
                                pe.wait_ge(hots, i * 2 + (par + 1))
                                products(par)
                        if NG % 2:
                            pe.wait_ge(hots, NG)
                            products(0)
                        pe.matmul(deg_ps[:, :], zeros[:, 0:P], zeros[:, 0:HIS], start=False, stop=True
                                  ).then_inc(summed, 1)
            end_stage()

        with ExitStack() as s:
            stage.append(s)
            SLICES = 5
            ST = NT // SLICES
            xs = sb("xs", [P, NT, P])
            degc = sb("degc", [P, NT])
            half = sb("half", [P, ST])
            rsq = sb("rsq", [P, NT])
            clamped, rooted, halves, dis_made = sem("clamped"), sem("rooted"), sem("halves"), sem("dis_made")
            x_in = [sem(f"x_in{k}") for k in range(SLICES)]
            y_made, y_out = sem("y_made"), sem("y_out")
            x_nodes = ins["x"].rearrange("(t p) f -> p t f", p=P)
            y_nodes = y_tab.rearrange("(t p) f -> p t f", p=P)
            with nc.Block() as block:
                @block.sync
                def _(sp):
                    for k in range(SLICES):
                        sp.dma_start(xs[:, k * ST:(k + 1) * ST, :], x_nodes[:, k * ST:(k + 1) * ST, :]
                                     ).then_inc(x_in[k], 16)
                    for k in range(SLICES):
                        sp.wait_ge(y_made, k + 1)
                        sp.dma_start(y_nodes[:, k * ST:(k + 1) * ST, :], xs[:, k * ST:(k + 1) * ST, :]
                                     ).then_inc(y_out, 16)
                    sp.wait_ge(y_out, 16 * SLICES)

                @block.gpsimd
                def _(pool):
                    pool.memset(half[:, :], -0.5).then_inc(halves, 1)
                    pool.wait_ge(halves, 1)
                    pool.wait_ge(clamped, 1)
                    for k in range(SLICES):
                        part = slice(k * ST, (k + 1) * ST)
                        pool.tensor_tensor(rsq[:, part], degc[:, part], half[:, :], ALU.pow).then_inc(rooted, 1)

                @block.vector
                def _(dve):
                    dve.tensor_scalar(degc[:, :], deg[:, :], 1.0, None, ALU.max).then_inc(clamped, 1)
                    for k in range(SLICES):
                        part = slice(k * ST, (k + 1) * ST)
                        dve.wait_ge(rooted, k + 1)
                        dve.scalar_tensor_tensor(out=dis[:, part], in0=deg[:, part], scalar=0.0, in1=rsq[:, part],
                                                 op0=ALU.is_gt, op1=ALU.mult).then_inc(dis_made, 1)
                        dve.wait_ge(dis_made, k + 1)
                        dve.wait_ge(x_in[k], 16)
                        dve.tensor_tensor(xs[:, part, :], xs[:, part, :],
                                          dis[:, part].unsqueeze(2).to_broadcast([P, ST, P]), ALU.mult
                                          ).then_inc(y_made, 1)
            end_stage()

        def done(c, g, before=0):
            return c * CG + (g + CG + 1 - before)

        def groups(last):
            return range(LG if last else CG)

        def window_done(c, before=0):
            return c + (CG + 1 - before)

        def scatter_buffers(tag, edge_product):
            b = {}
            if edge_product:
                b["wg"] = sb(tag + "wg", [R, P])
                b["attr"] = sb(tag + "attr", [R, CG, GE])
                b["prod"] = sb(tag + "prod", [P, 2, GE])
                b["filt_ps"] = ps(tag + "filt_ps", [P, 2, GE])
                b["window_in"] = sb(tag + "window_in", [P, P])
                b["window"] = sb(tag + "window", [P, P])
                b["hot"] = sb(tag + "hot", [P, 2, GE])
                b["values"] = sb(tag + "values", [P, 2, GE])
                b["wrows_ps"] = ps(tag + "wrows_ps", [P, GE])
                b["values_ps"] = ps(tag + "values_ps", [P, GE])
                b["wbase"] = sb(tag + "wbase", [P, 1])
            b["rows"] = sb(tag + "rows", [2, CG, 2, GE], BF16)
            b["gidx"] = sb(tag + "gidx", [P, CG, GT], I32)
            b["got"] = sb(tag + "got", [P, CG, GE])
            b["tcol"] = sb(tag + "tcol", [P, CT])
            b["same"] = sb(tag + "same", [P, 2, GE])
            b["earlier"] = sb(tag + "earlier", [P, 2, GT])
            b["shifted"] = sb(tag + "shifted", [P, CT])
            b["pick"] = sb(tag + "pick", [P, 2, GT])
            b["sidx"] = sb(tag + "sidx", [P, CG, GT], I32)
            b["summed"] = sb(tag + "summed", [P, CG, GE])
            b["rows_ps"] = ps(tag + "rows_ps", [P, 2, GE])
            b["sum_ps"] = ps(tag + "sum_ps", [P, 2, GE])
            for name in ("rows_in", "attr_in", "got_in"):
                b[name] = [sem(f"{tag}_{name}{g}") for g in range(CG)]
            b["acc_done"] = [sem(f"{tag}_acc_done{q}") for q in range(ACCS)]
            for name in ("w_in", "copies_cleared", "rows_made", "same_made", "counted", "columns", "filt_made", "prod_made",
                         "sums_made", "sums_out", "sidx_made", "gidx_made", "gather_passed", "scatter_passed",
                         "sync_passed", "window_ready", "window_taken", "window_set", "hot_made", "looked_up",
                         "values_out"):
                b[name] = sem(f"{tag}_{name}")
            return b

        def scatter_pass(b, table, gather_f, target, target_f, acc, edge_product, window):
            rows, gidx, got, tcol, same = b["rows"], b["gidx"], b["got"], b["tcol"], b["same"]
            earlier, shifted, pick, sidx, summed = b["earlier"], b["shifted"], b["pick"], b["sidx"], b["summed"]
            rows_ps, sum_ps = b["rows_ps"], b["sum_ps"]
            if edge_product:
                wg, attr, prod, filt_ps = b["wg"], b["attr"], b["prod"], b["filt_ps"]
            if window:
                window_in, window_sb, hot, values = b["window_in"], b["window"], b["hot"], b["values"]
                wrows_ps, values_ps, wbase = b["wrows_ps"], b["values_ps"], b["wbase"]
            acc_done = b["acc_done"]

            def sync(sp):
                if edge_product:
                    sp.dma_start(wg[:, :], ins["WgT"]).then_inc(b["w_in"], 16)
                def chunk(c, last):
                    if window:
                        base = sp.value_load(base_i[0:1, bass.ds(c, 1)], min_val=0, max_val=NROWS - P)
                        sp.wait_ge(b["window_taken"], c + 1)
                        sp.sem_inc(b["sync_passed"], 1)
                        sp.dma_start(window_in[:, :], table[bass.ds(base, P), :]).then_inc(b["window_ready"], 16)
                    for g in groups(last):
                        sp.wait_ge(b["rows_made"], done(c, g, CG))
                        sp.sem_inc(b["sync_passed"], 1)
                        sp.dma_start(rows[:, g, :, :], rows_tab[:, :, bass.ds(c * CE + g * GE, GE)]
                                     ).then_inc(b["rows_in"][g], 16)
                        if edge_product:
                            sp.wait_ge(b["filt_made"], done(c, g, CG))
                            sp.sem_inc(b["sync_passed"], 1)
                            sp.dma_start(attr[:, g, :], ins["attr_t"][:, bass.ds(c * CE + g * GE, GE)]
                                         ).then_inc(b["attr_in"][g], 16)

                with sp.Fori(0, CH - 1) as c:
                    chunk(c, False)
                chunk(CH - 1, True)

            def gpsimd(pool):
                def gather(c, g):
                    pool.wait_ge(b["gidx_made"], done(c, g))
                    pool.wait_ge(b["prod_made" if edge_product else "sums_made"], done(c, g, CG))
                    pool.sem_inc(b["gather_passed"], 1)
                    for k in range(GT):
                        pool.indirect_dma_start(
                            out=got[:, g, k * P:(k + 1) * P], out_offset=None, in_=table,
                            in_offset=bass.IndirectOffsetOnAxis(ap=gidx[:, g, k:k + 1], axis=0)
                        ).then_inc(b["got_in"][g], 16)

                def scatter(c, g, first):
                    pool.wait_ge(b["sums_out"], done(c, g))
                    pool.wait_ge(b["sidx_made"], done(c, g))
                    for k in range(GT):
                        t = g * GT + k
                        q = t % ACCS
                        if not (first and t < ACCS):
                            pool.wait_ge(acc_done[q], c * (CT // ACCS * 16) + (t // ACCS) * 16)
                        pool.sem_inc(b["scatter_passed"], 1)
                        pool.indirect_dma_start(
                            out=acc[q], out_offset=bass.IndirectOffsetOnAxis(ap=sidx[:, g, k:k + 1], axis=0),
                            in_=summed[:, g, k * P:(k + 1) * P], in_offset=None, compute_op=ALU.add
                        ).then_inc(acc_done[q], 16)

                def chunk(c, first, last):
                    for g in groups(last):
                        if not window:
                            if g + LAG < len(groups(last)):
                                gather(c, g + LAG)
                            elif not last:
                                gather(c + 1, g + LAG - CG)
                        scatter(c, g, first)

                pool.sem_inc(b["scatter_passed"], CT)
                if not window:
                    for g in range(LAG):
                        gather(0, g)
                chunk(0, True, CH == 1)
                if CH > 2:
                    with pool.Fori(1, CH - 1) as c:
                        chunk(c, False, False)
                if CH > 1:
                    chunk(CH - 1, False, True)
                for q in range(ACCS):
                    tiles = (CH - 1) * (CT // ACCS) + len(range(q, LG * GT, ACCS))
                    pool.wait_ge(acc_done[q], tiles * 16)

            def tensor(pe):
                pe.sem_inc(b["rows_made"], CG)
                pe.sem_inc(b["filt_made"], CG)
                pe.sem_inc(b["sums_made"], CG)
                pe.sem_inc(b["looked_up"], CG)
                if edge_product:
                    pe.wait_ge(b["w_in"], 16)

                def front(c, g):
                    h = g % 2
                    pe.wait_ge(b["rows_in"][g], c * 16 + 16)
                    if window:
                        pe.wait_ge(b["hot_made"], done(c, g, 1))
                        pe.matmul(wrows_ps[:, :], hilo_w[:, :], rows[:, g, 1 - target, :], start=True, stop=True)
                    pe.wait_ge(b["same_made"], done(c, g, 2))
                    pe.matmul(rows_ps[:, h, :], hilo_w[:, :], rows[:, g, target, :], start=True, stop=True
                              ).then_inc(b["rows_made"], 1)
                    if edge_product:
                        pe.wait_ge(b["attr_in"][g], c * 16 + 16)
                        pe.wait_ge(b["prod_made"], done(c, g, 2))
                        for k in range(GT):
                            col = slice(k * P, (k + 1) * P)
                            m = pe.matmul(filt_ps[:, h, col], attr[:, g, col], wg[:, :], start=True, stop=True)
                        m.then_inc(b["filt_made"], 1)

                def look_up(c, g):
                    h = g % 2
                    pe.wait_ge(b["window_set"], c + 1)
                    pe.wait_ge(b["hot_made"], done(c, g))
                    pe.wait_ge(b["values_out"], done(c, g, 1))
                    for k in range(GT):
                        col = slice(k * P, (k + 1) * P)
                        m = pe.matmul(values_ps[:, col], hot[:, h, col], window_sb[:, :], start=True, stop=True)
                    m.then_inc(b["looked_up"], 1)

                def back(c, g):
                    h = g % 2
                    pe.wait_ge(b["same_made"], done(c, g))
                    pe.wait_ge(b["sums_out"], done(c, g, 2))
                    if edge_product:
                        pe.wait_ge(b["prod_made"], done(c, g))
                        terms = prod[:, h, :]
                    else:
                        pe.wait_ge(b["got_in"][g], c * (GT * 16) + GT * 16)
                        terms = got[:, g, :]
                    for k in range(GT):
                        col = slice(k * P, (k + 1) * P)
                        m = pe.matmul(sum_ps[:, h, col], same[:, h, col], terms[:, col], start=True, stop=True)
                    m.then_inc(b["sums_made"], 1)

                def chunk(c, last):
                    for g in groups(last):
                        nxt = (c, g + 1) if g + 1 < len(groups(last)) else None if last else (c + 1, 0)
                        if nxt:
                            front(*nxt)
                        back(c, g)
                        if nxt and window:
                            look_up(*nxt)

                front(0, 0)
                if window:
                    look_up(0, 0)
                with pe.Fori(0, CH - 1) as c:
                    chunk(c, False)
                chunk(CH - 1, True)

            def vector(dve):
                dve.sem_inc(b["same_made"], CG)
                dve.sem_inc(b["prod_made"], CG)
                dve.sem_inc(b["gidx_made"], CG)
                dve.sem_inc(b["hot_made"], CG)
                if not window:
                    for g in range(CG):
                        dve.tensor_copy(gidx[:, g, :], gather_f[:, g * GT:(g + 1) * GT]).then_inc(b["gidx_made"], 1)

                def chunk(c, last):
                    if window:
                        dve.tensor_copy(wbase[:, :], base_p[:, bass.ds(c, 1)])
                    dve.tensor_copy(tcol[:, :], target_f[:, bass.ds(c * CT, CT)]).then_inc(b["columns"], 1)
                    dve.wait_ge(b["columns"], c * 2 + 1)
                    dve.tensor_scalar(shifted[:, :], tcol[:, :], spare_row[:, 0:1], None,
                                      ALU.subtract).then_inc(b["columns"], 1)
                    dve.wait_ge(b["columns"], c * 2 + 2)
                    for g in groups(last):
                        h = g % 2
                        dve.wait_ge(b["rows_made"], done(c, g))
                        if window:
                            dve.wait_ge(b["looked_up"], done(c, g, 2))
                            dve.tensor_scalar(hot[:, h, :], wrows_ps[:, :], wbase[:, 0:1], None, ALU.is_equal
                                              ).then_inc(b["hot_made"], 1)
                        dve.wait_ge(b["sums_made"], done(c, g, 2))
                        for k in range(GT):
                            col = slice(k * P, (k + 1) * P)
                            t = g * GT + k
                            m = dve.scalar_tensor_tensor(
                                out=same[:, h, col], in0=rows_ps[:, h, col], scalar=tcol[:, t:t + 1],
                                in1=not_earlier[:, :], op0=ALU.is_equal, op1=ALU.mult,
                                accum_out=earlier[:, h, k:k + 1])
                        m.then_inc(b["counted"], 1)
                        dve.wait_ge(b["counted"], c * CG + (g + 1))
                        dve.wait_ge(b["sidx_made"], done(c, g, 2))
                        dve.scalar_tensor_tensor(
                            out=pick[:, h, :], in0=earlier[:, h, :], scalar=1.5,
                            in1=shifted[:, g * GT:(g + 1) * GT], op0=ALU.is_lt, op1=ALU.mult
                        ).then_inc(b["same_made"], 1)
                        if not window and (edge_product or not last):
                            dve.wait_ge(b["got_in"][g], c * (GT * 16) + GT * 16)
                        if edge_product:
                            dve.wait_ge(b["filt_made"], done(c, g))
                            if window:
                                dve.wait_ge(b["values_out"], done(c, g))
                            terms = values[:, h, :] if window else got[:, g, :]
                            dve.tensor_tensor(prod[:, h, :], filt_ps[:, h, :], terms, ALU.mult
                                              ).then_inc(b["prod_made"], 1)
                        if not window and not last:
                            dve.tensor_copy(gidx[:, g, :], gather_f[:, bass.ds(c * CT + (CT + g * GT), GT)]
                                            ).then_inc(b["gidx_made"], 1)

                with dve.Fori(0, CH - 1) as c:
                    chunk(c, False)
                chunk(CH - 1, True)

            def scalar(act):
                act.sem_inc(b["sums_out"], CG)
                act.sem_inc(b["sidx_made"], CG)
                act.sem_inc(b["values_out"], CG)
                act.sem_inc(b["window_taken"], 1)
                def chunk(c, last):
                    for g in groups(last):
                        h = g % 2
                        if window:
                            if g == 0:
                                act.wait_ge(b["window_ready"], c * 16 + 16)
                                act.wait_ge(b["looked_up"], done(c, g, 1))
                                act.copy(window_sb[:, :], window_in[:, :]).then_inc(b["window_set"], 1)
                                act.wait_ge(b["window_set"], c + 1)
                                act.sem_inc(b["window_taken"], 1)
                            act.wait_ge(b["looked_up"], done(c, g))
                            act.wait_ge(b["prod_made"], done(c, g, 2))
                            act.copy(values[:, h, :], values_ps[:, :]).then_inc(b["values_out"], 1)
                        act.wait_ge(b["scatter_passed"], c * CT + (g * GT + GT + ACCS))
                        act.wait_ge(b["same_made"], done(c, g))
                        act.activation(sidx[:, g, :], pick[:, h, :], ACT.Identity,
                                       bias=spare_row[:, 0:1]).then_inc(b["sidx_made"], 1)
                        act.wait_ge(b["sums_made"], done(c, g))
                        act.copy(summed[:, g, :], sum_ps[:, h, :]).then_inc(b["sums_out"], 1)

                with act.Fori(0, CH - 1) as c:
                    chunk(c, False)
                chunk(CH - 1, True)

            return sync, gpsimd, tensor, vector, scalar

        conv_scope = ctx.enter_context(ExitStack())
        stage.append(conv_scope)
        conv_sums = sb("conv_sums", [P, NT, P])
        stage.pop()

        with ExitStack() as s:
            stage.append(s)
            TURN = 2
            b = scatter_buffers("conv", False)
            any_sync, any_pool, any_pe, any_dve, any_act = scatter_pass(
                b, y_tab, src_f, 1, dst_f, conv_acc, False, False)
            win_ps = ps("win_ps", [P, P])
            win = sb("win", [P, P])
            place = sb("place", [P, 3])
            turn = sb("turn", [P, 2, P])
            turned_ps = ps("turned_ps", [P, 2, P])
            rcol = sb("rcol", [P, CT])
            win_out, win_added, merged, fetched = sem("win_out"), sem("win_added"), sem("merged"), sem("fetched")
            placed, turn_made, turned, sums_cleared = sem("placed"), sem("turn_made"), sem("turned"), sem("sums_cleared")

            with nc.Block() as block:
                @block.sync
                def _(sp):
                    with sp.If(fits_here(sp)):
                        sp.nop()
                    with sp.Else():
                        any_sync(sp)

                @block.gpsimd
                def _(pool):
                    def gather(c, g):
                        pool.wait_ge(b["gidx_made"], done(c, g))
                        pool.wait_ge(b["sums_made"], done(c, g, CG))
                        pool.sem_inc(b["gather_passed"], 1)
                        for k in range(GT):
                            pool.indirect_dma_start(
                                out=b["got"][:, g, k * P:(k + 1) * P], out_offset=None, in_=y_tab,
                                in_offset=bass.IndirectOffsetOnAxis(ap=b["gidx"][:, g, k:k + 1], axis=0)
                            ).then_inc(b["got_in"][g], 16)

                    with pool.If(fits_here(pool)):
                        for g in range(CG):
                            gather(0, g)

                        with pool.Fori(1, CH - 1) as c:
                            for g in range(CG):
                                gather(c, g)
                        for g in groups(True):
                            gather(CH - 1, g)
                    with pool.Else():
                        for q in range(1, ACCS):
                            clear(pool, conv_acc[q], b["copies_cleared"])
                        pool.wait_ge(b["copies_cleared"], (ACCS - 1) * 16)
                        any_pool(pool)
                        for q in range(1, ACCS):
                            pool.dma_start(conv_acc[0].rearrange("(p a) f -> p (a f)", p=P),
                                           conv_acc[q].rearrange("(p a) f -> p (a f)", p=P),
                                           accum_op=ALU.add, max_dma_last_dim=4 * 2048).then_inc(merged, 16)
                            pool.wait_ge(merged, q * 16)
                        pool.dma_start(conv_sums[:, :, :], conv_acc[0].rearrange("(t p) f -> p t f", p=P)
                                       ).then_inc(fetched, 16)
                        pool.wait_ge(fetched, 16)

                @block.tensor
                def _(pe):
                    def turn_window(c):
                        pe.wait_ge(win_out, window_done(c))
                        pe.wait_ge(turn_made, c + 1)
                        pe.wait_ge(win_added, c + 1)
                        for k in range(2):
                            m = pe.matmul(turned_ps[:, k, :], turn[:, k, :], win[:, :], start=True, stop=True)
                        m.then_inc(turned, 1)

                    with pe.If(fits_here(pe)):
                        pe.sem_inc(b["sums_made"], CG)
                        pe.sem_inc(turned, 1)

                        def chunk(c, first, last):
                            for g in groups(last):
                                if g == TURN and not first:
                                    turn_window(c - 1)
                                h = g % 2
                                pe.wait_ge(b["hot_made"], done(c, g))
                                pe.wait_ge(b["got_in"][g], c * (GT * 16) + GT * 16)
                                if g == 0:
                                    pe.wait_ge(win_out, window_done(c, 1))
                                for k in range(GT):
                                    col = slice(k * P, (k + 1) * P)
                                    m = pe.matmul(win_ps[:, :], b["same"][:, h, col], b["got"][:, g, col],
                                                  start=g == 0 and k == 0,
                                                  stop=g == groups(last)[-1] and k == GT - 1)
                                m.then_inc(b["sums_made"], 1)

                        chunk(0, True, False)
                        with pe.Fori(1, CH - 1) as c:
                            chunk(c, False, False)
                        chunk(CH - 1, False, True)
                        turn_window(CH - 1)
                    with pe.Else():
                        any_pe(pe)

                @block.vector
                def _(dve):
                    with dve.If(fits_here(dve)):
                        dve.sem_inc(b["gidx_made"], CG)
                        dve.sem_inc(b["hot_made"], CG)
                        dve.sem_inc(win_added, 1)
                        for g in range(CG):
                            dve.tensor_copy(b["gidx"][:, g, :], src_f[:, g * GT:(g + 1) * GT]
                                            ).then_inc(b["gidx_made"], 1)
                        dve.memset(conv_sums[:, :, :], 0.0).then_inc(sums_cleared, 1)
                        dve.wait_ge(sums_cleared, 1)

                        def make_turn(c):
                            dve.wait_ge(turned, c + 1)
                            dve.tensor_copy(place[:, :].unsqueeze(1), window_place[:, bass.ds(c, 1), :]
                                            ).then_inc(placed, 1)
                            dve.wait_ge(placed, c + 1)
                            for k in range(2):
                                m = dve.tensor_scalar(turn[:, k, :], iota[:, :], place[:, 0:1],
                                                      place[:, 1 + k:2 + k], ALU.is_equal, ALU.mult)
                            m.then_inc(turn_made, 1)

                        def add_window(c):
                            dve.wait_ge(turned, c + 2)
                            block_ = dve.value_load(window_block[0:1, bass.ds(c, 1)], min_val=0, max_val=NT - 2)
                            dve.wait_ge(win_added, c + 1)
                            two = conv_sums[:, bass.ds(block_, 2), :]
                            dve.tensor_tensor(two, turned_ps[:, :, :], two, ALU.add).then_inc(win_added, 1)

                        def chunk(c, first, last):
                            dve.wait_ge(b["hot_made"], done(c, 0, 1))
                            dve.tensor_copy(rcol[:, :], in_window[:, bass.ds(c * CT, CT)]).then_inc(b["columns"], 1)
                            dve.wait_ge(b["columns"], c + 1)
                            for g in groups(last):
                                h = g % 2
                                if g == TURN:
                                    if not first:
                                        add_window(c - 1)
                                    make_turn(c)
                                dve.wait_ge(b["sums_made"], done(c, g, 2))
                                for k in range(GT):
                                    t = g * GT + k
                                    m = dve.tensor_scalar(b["same"][:, h, k * P:(k + 1) * P], iota[:, :],
                                                          rcol[:, t:t + 1], None, ALU.is_equal)
                                m.then_inc(b["hot_made"], 1)
                                if not last:
                                    dve.wait_ge(b["got_in"][g], c * (GT * 16) + GT * 16)
                                    dve.tensor_copy(b["gidx"][:, g, :], src_f[:, bass.ds(c * CT + (CT + g * GT), GT)]
                                                    ).then_inc(b["gidx_made"], 1)

                        chunk(0, True, False)
                        with dve.Fori(1, CH - 1) as c:
                            chunk(c, False, False)
                        chunk(CH - 1, False, True)
                        add_window(CH - 1)
                    with dve.Else():
                        any_dve(dve)

                @block.scalar
                def _(act):
                    with act.If(fits_here(act)):
                        act.sem_inc(win_out, CG)


                        def chunk(c, last):
                            act.wait_ge(b["sums_made"], done(c, groups(last)[-1]))
                            act.wait_ge(turned, c + 1)
                            act.copy(win[:, :], win_ps[:, :]).then_inc(win_out, 1)

                        with act.Fori(0, CH - 1) as c:
                            chunk(c, False)
                        chunk(CH - 1, True)
                    with act.Else():
                        any_act(act)
            end_stage()

        WI, WJ, W1, W2, WV = 0, 1, 2, 5, 8
        BI, B1, B2, BV, GATE = 0, 1, 4, 7, 8
        CAP = 40.0
        EPS = 1e-5
        ROUNDS = BLOCKS // STREAMS
        streams = range(STREAMS)

        TEAMS = (range(0, 3), range(3, STREAMS))

        def team_of(h):
            return int(h in TEAMS[1])

        def nth(i, h, many=1, k=0):
            team = TEAMS[team_of(h)]
            return i * (len(team) * many) + (len(team) * k + h - team[0] + 1)

        def since(i, h):
            return nth(i, h) + len(TEAMS[team_of(h)])

        def last_round(i, h):
            return nth(i, h)

        def block_rows(i, h):
            return bass.ds(i * (STREAMS * NB) + h * NB, NB)

        def by_node(tab):
            return tab.rearrange("(j p) f -> p j f", p=P)

        def split(buf):
            return buf.rearrange("p (j f) -> p j f", f=P)

        def in_turns(eng, steps, half, step):
            def turn(i, team, part, last):
                return [(i, team) + s_ + (last,) for s_ in (steps[half:] if part else steps[:half])]

            def mixed(ahead, behind):
                for n in range(max(len(ahead), len(behind))):
                    for side in (ahead, behind):
                        if n < len(side):
                            step(*side[n])

            mixed(turn(0, 0, 0, ROUNDS == 1), [])
            if ROUNDS > 1:
                with eng.Fori(0, ROUNDS - 1) as i:
                    mixed(turn(i, 0, 1, False), turn(i, 1, 0, False))
                    mixed(turn(i + 1, 0, 0, False), turn(i, 1, 1, False))
            mixed(turn(ROUNDS - 1, 0, 1, True), turn(ROUNDS - 1, 1, 0, True))
            mixed([], turn(ROUNDS - 1, 1, 1, True))

        with ExitStack() as s:
            stage.append(s)
            wts = sb("n1wts", [P, 2, P])
            cols = sb("n1cols", [P, 9])
            bj_rest = sb("n1bj", [1, 3, P])
            bj_parts = sb("n1bj_parts", [1, 3, P], BF16)
            ones_b = sb("n1ones", [1, P], BF16)
            xin = sb("n1xin", [P, STREAMS, NB])
            hid = sb("n1hid", [P, STREAMS, NB])
            x1 = sb("n1x1", [P, STREAMS, NB])
            xT = sb("n1xT", [P, STREAMS, NB])
            low = sb("n1low", [P, STREAMS, NB])
            v_sb = sb("n1v", [P, STREAMS, NB])
            u_sb = sb("n1u", [P, STREAMS, NB])
            stats = sb("n1stats", [P, STREAMS, 4, 6])
            mv = sb("n1mv", [P, STREAMS, 4, 2])
            var = sb("n1var", [P, STREAMS, 4])
            rstd = sb("n1rstd", [P, STREAMS, 4])
            half4 = sb("n1half", [P, 4])
            mm_ps = [ps(f"n1mm{h}", [P, NB]) for h in streams]
            sm = {k: [sem(f"n1_{k}{team}") for team in range(2)] for k in (
                "scaled", "joined", "stats", "mv", "var", "rstd", "x1", "low", "ex", "ln", "sp", "xTps", "xT",
                "mm", "v")}
            w_in = sem("n1_w_in")
            half_made = sem("n1_half_made")
            bj_split = sem("n1_bj_split")
            sync_passed = sem("n1_sync_passed")
            loaded = [sem(f"n1_loaded{h}") for h in streams]
            stores = [sem(f"n1_stores{h}") for h in streams]
            SOFTS = 3

            STEPS = [("scale", 0), ("join", 0), ("stats", 0), ("mean", 0), ("norm", 0), ("log", 0), ("X", 0), ("wait", 0),
                     ("log", 1), ("u", 0), ("wait", 1), ("log", 2), ("V", 0)]
            HALF = len(STEPS) // 2

            with nc.Block() as block:
                @block.sync
                def _(sp):
                    sp.dma_start(wts[:, :, :], ins["WT"][:, WI:WI + 2, :]).then_inc(w_in, 16)
                    sp.dma_start(cols[:, :], ins["cols"]).then_inc(w_in, 16)
                    sp.dma_start(bj_rest[:, 0, :], ins["bj"]).then_inc(w_in, 16)

                    def load(i, h):
                        at = block_rows(i, h)
                        sp.dma_start(split(xin[:, h, :]), by_node(ins["x"][at, :])).then_inc(loaded[h], 16)

                    def step(i, team, name, k, last):
                        for h in TEAMS[team]:
                            if name == "X":
                                if not last:
                                    sp.wait_ge(sm["joined"][team], nth(i, h))
                                    sp.sem_inc(sync_passed, 1)
                                    load(i + 1, h)
                                sp.wait_ge(sm["x1"][team], nth(i, h))
                                sp.sem_inc(sync_passed, 1)
                                sp.dma_start(by_node(x1_tab[block_rows(i, h), :]), split(x1[:, h, :])
                                             ).then_inc(stores[h], 16)
                            elif name == "u":
                                sp.wait_ge(sm["xT"][team], nth(i, h))
                                sp.sem_inc(sync_passed, 1)
                                sp.dma_start(xT_tab[:, block_rows(i, h)], xT[:, h, :]).then_inc(stores[h], 16)
                                sp.wait_ge(sm["sp"][team], nth(i, h, 2, 1))
                                sp.sem_inc(sync_passed, 1)
                                sp.dma_start(uT_tab[:, block_rows(i, h)], u_sb[:, h, :]).then_inc(stores[h], 16)
                            elif name == "V":
                                sp.wait_ge(sm["v"][team], since(i, h))
                                sp.sem_inc(sync_passed, 1)
                                sp.dma_start(by_node(v_tab[block_rows(i, h), :]), split(v_sb[:, h, :])
                                             ).then_inc(stores[h], 16)

                    for h in streams:
                        sp.sem_inc(stores[h], 16)
                        load(0, h)
                    in_turns(sp, STEPS, HALF, step)
                    for h in streams:
                        sp.wait_ge(stores[h], ROUNDS * 64 + 16)

                @block.gpsimd
                def _(pool):
                    def step(i, team, name, k, last):
                        if name == "mean":
                            for h in TEAMS[team]:
                                pool.wait_ge(sm["var"][team], nth(i, h))
                                pool.tensor_tensor(rstd[:, h, :], var[:, h, :], half4[:, :], ALU.pow
                                                   ).then_inc(sm["rstd"][team], 1)

                    pool.memset(half4[:, :], -0.5).then_inc(half_made, 1)
                    pool.wait_ge(half_made, 1)
                    in_turns(pool, STEPS, HALF, step)

                @block.vector
                def _(dve):
                    def step(i, team, name, k, last):
                        for h in TEAMS[team]:
                            if name == "scale":
                                dve.wait_ge(loaded[h], i * 16 + 16)
                                dve.wait_ge(sm["v"][team], last_round(i, h))
                                tiles = bass.ds(i * (STREAMS * 4) + h * 4, 4)
                                d = dis[:, tiles].unsqueeze(2).to_broadcast([P, 4, P])
                                dve.tensor_tensor(split(hid[:, h, :]), conv_sums[:, tiles, :], d, ALU.mult
                                                  ).then_inc(sm["scaled"][team], 1)
                            elif name == "join":
                                dve.wait_ge(sm["scaled"][team], nth(i, h))
                                dve.scalar_tensor_tensor(out=hid[:, h, :], in0=hid[:, h, :], scalar=0.0,
                                                         in1=xin[:, h, :], op0=ALU.max, op1=ALU.add
                                                         ).then_inc(sm["joined"][team], 1)
                            elif name == "stats":
                                dve.wait_ge(sm["joined"][team], nth(i, h))
                                for j in range(4):
                                    m = dve.bn_stats(stats[:, h, j, :], hid[:, h, j * P:(j + 1) * P])
                                m.then_inc(sm["stats"][team], 1)
                            elif name == "mean":
                                dve.wait_ge(sm["stats"][team], 1)
                                dve.wait_ge(sm["stats"][team], nth(i, h))
                                for j in range(4):
                                    m = dve.bn_aggr(mv[:, h, j, :], stats[:, h, j, :])
                                m.then_inc(sm["mv"][team], 1)
                            elif name == "norm":
                                dve.wait_ge(sm["rstd"][team], nth(i, h))
                                dve.wait_ge(stores[h], i * 64 + 16)
                                for j in range(4):
                                    col = slice(j * P, (j + 1) * P)
                                    m = dve.tensor_scalar(x1[:, h, col], hid[:, h, col], mv[:, h, j, 0:1],
                                                          rstd[:, h, j:j + 1], ALU.subtract, ALU.mult)
                                m.then_inc(sm["x1"][team], 1)
                            elif name == "log" and k == 0:
                                dve.wait_ge(sm["x1"][team], nth(i, h))
                                dve.tensor_scalar(low[:, h, :], x1[:, h, :], CAP, None, ALU.min
                                                  ).then_inc(sm["low"][team], 1)
                            elif name == "log":
                                dve.wait_ge(sm["mm"][team], nth(i, h, 2, k - 1))
                                if k == 1:
                                    dve.tensor_scalar(low[:, h, :], mm_ps[h][:, :], cols[:, BI:BI + 1], CAP,
                                                      ALU.add, ALU.min).then_inc(sm["low"][team], 1)
                                else:
                                    dve.tensor_scalar(low[:, h, :], mm_ps[h][:, :], CAP, None, ALU.min
                                                      ).then_inc(sm["low"][team], 1)
                            elif name == "X":
                                dve.wait_ge(sm["ln"][team], nth(i, h, SOFTS, 0))
                                dve.tensor_tensor(hid[:, h, :], x1[:, h, :], low[:, h, :], ALU.max
                                                  ).then_inc(sm["sp"][team], 1)
                            elif name == "u":
                                dve.wait_ge(sm["ln"][team], nth(i, h, SOFTS, 1))
                                dve.scalar_tensor_tensor(out=u_sb[:, h, :], in0=mm_ps[h][:, :],
                                                         scalar=cols[:, BI:BI + 1], in1=low[:, h, :],
                                                         op0=ALU.add, op1=ALU.max).then_inc(sm["sp"][team], 1)
                            elif name == "V":
                                dve.wait_ge(sm["ln"][team], nth(i, h, SOFTS, 2))
                                dve.tensor_tensor(v_sb[:, h, :], mm_ps[h][:, :], low[:, h, :], ALU.max
                                                  ).then_inc(sm["v"][team], 1)
                        if name == "mean":
                            for h in TEAMS[team]:
                                dve.wait_ge(sm["mv"][team], nth(i, h))
                                dve.tensor_scalar(var[:, h, :], mv[:, h, :, 1], EPS, None, ALU.add
                                                  ).then_inc(sm["var"][team], 1)

                    dve.memset(ones_b[:, :], 1.0)
                    dve.wait_ge(w_in, 48)
                    for n in range(3):
                        dve.tensor_copy(bj_parts[:, n, :], bj_rest[:, n, :]).then_inc(bj_split, 1)
                        dve.wait_ge(bj_split, 2 * n + 1)
                        if n < 2:
                            dve.tensor_tensor(bj_rest[:, n + 1, :], bj_rest[:, n, :], bj_parts[:, n, :],
                                              ALU.subtract).then_inc(bj_split, 1)
                            dve.wait_ge(bj_split, 2 * n + 2)
                    for team in range(2):
                        dve.sem_inc(sm["v"][team], len(TEAMS[team]))
                    in_turns(dve, STEPS, HALF, step)

                @block.scalar
                def _(act):
                    def step(i, team, name, k, last):
                        if name == "log":
                            for h in TEAMS[team]:
                                act.wait_ge(sm["low"][team], nth(i, h, SOFTS, k))
                                act.activation(low[:, h, :], low[:, h, :], ACT.Exp).then_inc(sm["ex"][team], 1)
                            for h in TEAMS[team]:
                                act.wait_ge(sm["ex"][team], nth(i, h, SOFTS, k))
                                act.activation(low[:, h, :], low[:, h, :], ACT.Ln, bias=1.0
                                               ).then_inc(sm["ln"][team], 1)
                        if name == "X":
                            for h in TEAMS[team]:
                                act.wait_ge(sm["xTps"][team], nth(i, h))
                                act.wait_ge(stores[h], i * 64 + 16)
                                act.copy(xT[:, h, :], mm_ps[h][:, :]).then_inc(sm["xT"][team], 1)

                    act.wait_ge(w_in, 48)
                    act.preload_act_table_set("natural_log_exp_and_others")
                    in_turns(act, STEPS, HALF, step)

                @block.tensor
                def _(pe):
                    def step(i, team, name, k, last):
                        if name == "X":
                            for h in TEAMS[team]:
                                pe.wait_ge(sm["sp"][team], nth(i, h, 2, 0))
                                pe.wait_ge(sm["v"][team], last_round(i, h))
                                for j in range(4):
                                    col = slice(j * P, (j + 1) * P)
                                    m = pe.transpose(mm_ps[h][:, col], hid[:, h, col], ident[:, :])
                                m.then_inc(sm["xTps"][team], 1)
                            for h in TEAMS[team]:
                                pe.wait_ge(sm["xT"][team], nth(i, h))
                                pe.matmul(mm_ps[h][:, :], wts[:, WI, :], xT[:, h, :], start=True, stop=True
                                          ).then_inc(sm["mm"][team], 1)
                        if name == "u":
                            for h in TEAMS[team]:
                                pe.wait_ge(sm["sp"][team], nth(i, h, 2, 1))
                                for n in range(3):
                                    pe.matmul(split(mm_ps[h][:, :]), ones_b[:, :],
                                              bj_parts[:, n, :].unsqueeze(1).to_broadcast([1, 4, P]),
                                              start=n == 0, stop=False)
                                for j in range(4):
                                    col = slice(j * P, (j + 1) * P)
                                    m = pe.matmul(mm_ps[h][:, col], xT[:, h, col], wts[:, WJ, :], start=False,
                                                  stop=j == 3)
                                m.then_inc(sm["mm"][team], 1)

                    pe.wait_ge(w_in, 48)
                    pe.wait_ge(bj_split, 5)
                    in_turns(pe, STEPS, HALF, step)
            end_stage()

        conv_scope.close()

        with ExitStack() as s:
            stage.append(s)
            b = scatter_buffers("pair", True)
            windowed = scatter_pass(b, v_tab, dst_f, 0, src_f, pair_acc, True, True)
            gathered = scatter_pass(b, v_tab, dst_f, 0, src_f, pair_acc, True, False)
            with nc.Block() as block:
                @block.sync
                def _(sp):
                    with sp.If(fits_here(sp)):
                        windowed[0](sp)
                    with sp.Else():
                        gathered[0](sp)

                @block.gpsimd
                def _(pool):
                    with pool.If(fits_here(pool)):
                        windowed[1](pool)
                    with pool.Else():
                        gathered[1](pool)

                @block.tensor
                def _(pe):
                    with pe.If(fits_here(pe)):
                        windowed[2](pe)
                    with pe.Else():
                        gathered[2](pe)

                @block.vector
                def _(dve):
                    with dve.If(fits_here(dve)):
                        windowed[3](dve)
                    with dve.Else():
                        gathered[3](dve)

                @block.scalar
                def _(act):
                    with act.If(fits_here(act)):
                        windowed[4](act)
                    with act.Else():
                        gathered[4](act)
            end_stage()

        edge_scope.close()

        with ExitStack() as s:
            stage.append(s)
            wts = sb("n2wts", [P, 9, P])
            cols = sb("n2cols", [P, 9])
            pair = sb("n2pair", [P, STREAMS, NB])
            x1 = sb("n2x1", [P, STREAMS, NB])
            xT = sb("n2xT", [P, STREAMS, NB])
            u0 = sb("n2u0", [P, STREAMS, NB])
            u = sb("n2u", [P, STREAMS, NB])
            low = sb("n2low", [P, STREAMS, NB])
            sp_u = sb("n2sp", [P, STREAMS, NB])
            gx = sb("n2gx", [P, STREAMS, NB])
            res = sb("n2res", [P, STREAMS, NB])
            stats = sb("n2stats", [P, STREAMS, 4, 6])
            mv = sb("n2mv", [P, STREAMS, 4, 2])
            var = sb("n2var", [P, STREAMS, 4])
            rstd = sb("n2rstd", [P, STREAMS, 4])
            half4 = sb("n2half", [P, 4])
            mm_ps = [ps(f"n2mm{h}", [P, NB]) for h in streams]
            sm2 = {k: [sem(f"n2_{k}{team}") for team in range(2)] for k in (
                "summed", "low", "ex", "ln", "sp", "mm", "u", "gx", "joined", "stats", "mv", "var",
                "rstd", "res")}
            w_in = sem("n2_w_in")
            sync_passed = sem("n2_sync_passed")
            pool_passed = sem("n2_pool_passed")
            half_made = sem("n2_half_made")
            pair_in = [sem(f"n2_pair_in{h}") for h in streams]
            loaded = [sem(f"n2_loaded{h}") for h in streams]
            stores = [sem(f"n2_stores{h}") for h in streams]
            SOFTS = 7

            STEPS = [("sum", 0)]
            for k in range(SOFTS):
                STEPS += [("log", k), ("max", k)] + [("wait", k)] * (1 - k % 2) + [("residual", k)] * (k % 2)
            STEPS += [("join", 0), ("stats", 0), ("mean", 0), ("result", 0)]
            HALF = len(STEPS) // 2

            with nc.Block() as block:
                @block.sync
                def _(sp):
                    sp.dma_start(wts[:, :, :], ins["WT"]).then_inc(w_in, 16)
                    sp.dma_start(cols[:, :], ins["cols"]).then_inc(w_in, 16)

                    def load(i, h):
                        at = block_rows(i, h)
                        sp.dma_start(split(x1[:, h, :]), by_node(x1_tab[at, :])).then_inc(loaded[h], 16)
                        sp.dma_start(xT[:, h, :], xT_tab[:, at]).then_inc(loaded[h], 16)
                        sp.dma_start(u0[:, h, :], uT_tab[:, at]).then_inc(loaded[h], 16)

                    def step(i, team, name, k, last):
                        if name == "join" and not last:
                            for h in TEAMS[team]:
                                sp.wait_ge(sm2["joined"][team], nth(i, h))
                                sp.sem_inc(sync_passed, 1)
                                load(i + 1, h)
                        if name == "result":
                            for h in TEAMS[team]:
                                sp.wait_ge(sm2["res"][team], since(i, h))
                                sp.sem_inc(sync_passed, 1)
                                sp.dma_start(by_node(out[block_rows(i, h), :]), split(res[:, h, :])
                                             ).then_inc(stores[h], 16)

                    for h in streams:
                        sp.sem_inc(stores[h], 16)
                        load(0, h)
                    in_turns(sp, STEPS, HALF, step)
                    for h in streams:
                        sp.wait_ge(stores[h], ROUNDS * 16 + 16)

                @block.gpsimd
                def _(pool):
                    def add_copy(i, h, q, before):
                        if q == 0 and before is not None:
                            pool.wait_ge(sm2["summed"][team_of(h)], nth(before, h))
                        if q:
                            pool.wait_ge(pair_in[h], i * (16 * ACCS) + q * 16)
                        if q or before is not None:
                            pool.sem_inc(pool_passed, 1)
                        src_at = by_node(pair_acc[q][block_rows(i, h), :])
                        if q:
                            m = pool.dma_start(split(pair[:, h, :]), src_at, accum_op=ALU.add)
                        else:
                            m = pool.dma_start(split(pair[:, h, :]), src_at)
                        m.then_inc(pair_in[h], 16)

                    def step(i, team, name, k, last):
                        q = STEPS.index((name, k)) - HALF
                        if 0 <= q < ACCS and not last:
                            for h in TEAMS[team]:
                                add_copy(i + 1, h, q, i)
                        if name == "mean":
                            for h in TEAMS[team]:
                                pool.wait_ge(sm2["var"][team], nth(i, h))
                                pool.tensor_tensor(rstd[:, h, :], var[:, h, :], half4[:, :], ALU.pow
                                                   ).then_inc(sm2["rstd"][team], 1)

                    pool.memset(half4[:, :], -0.5).then_inc(half_made, 1)
                    pool.wait_ge(half_made, 1)
                    for team in range(2):
                        for q in range(ACCS):
                            for h in TEAMS[team]:
                                add_copy(0, h, q, None)
                    in_turns(pool, STEPS, HALF, step)

                @block.vector
                def _(dve):
                    def step(i, team, name, k, last):
                        layer = k // 2
                        inner = k % 2 == 1
                        for h in TEAMS[team]:
                            if name == "sum":
                                dve.wait_ge(loaded[h], i * 48 + 48)
                                dve.wait_ge(sm2["summed"][team], nth(i, h))
                                dve.wait_ge(sm2["res"][team], last_round(i, h))
                                dve.tensor_tensor(u[:, h, :], u0[:, h, :], mm_ps[h][:, :], ALU.add
                                                  ).then_inc(sm2["u"][team], 1)
                            elif name == "log" and inner:
                                dve.wait_ge(sm2["mm"][team], nth(i, h, SOFTS, k - 1))
                                dve.tensor_scalar(low[:, h, :], mm_ps[h][:, :], cols[:, B1 + layer:B1 + layer + 1],
                                                  CAP, ALU.add, ALU.min).then_inc(sm2["low"][team], 1)
                            elif name == "log":
                                dve.wait_ge(sm2["u"][team], nth(i, h, 4, layer))
                                dve.tensor_scalar(low[:, h, :], u[:, h, :], CAP, None, ALU.min
                                                  ).then_inc(sm2["low"][team], 1)
                            elif name == "max" and inner:
                                dve.wait_ge(sm2["ln"][team], nth(i, h, SOFTS, k))
                                dve.scalar_tensor_tensor(out=sp_u[:, h, :], in0=mm_ps[h][:, :],
                                                         scalar=cols[:, B1 + layer:B1 + layer + 1],
                                                         in1=low[:, h, :], op0=ALU.add, op1=ALU.max
                                                         ).then_inc(sm2["sp"][team], 1)
                            elif name == "max":
                                dve.wait_ge(sm2["ln"][team], nth(i, h, SOFTS, k))
                                dve.tensor_tensor(sp_u[:, h, :], u[:, h, :], low[:, h, :], ALU.max
                                                  ).then_inc(sm2["sp"][team], 1)
                            elif name == "residual":
                                dve.wait_ge(sm2["mm"][team], nth(i, h, SOFTS, k))
                                dve.scalar_tensor_tensor(out=u[:, h, :], in0=mm_ps[h][:, :],
                                                         scalar=cols[:, B2 + layer:B2 + layer + 1],
                                                         in1=u[:, h, :], op0=ALU.add, op1=ALU.add
                                                         ).then_inc(sm2["u"][team], 1)
                            elif name == "join":
                                dve.wait_ge(sm2["mm"][team], nth(i, h, SOFTS, 6))
                                dve.tensor_tensor(u[:, h, :], mm_ps[h][:, :], x1[:, h, :], ALU.add
                                                  ).then_inc(sm2["joined"][team], 1)
                            elif name == "stats":
                                dve.wait_ge(sm2["joined"][team], nth(i, h))
                                for j in range(4):
                                    m = dve.bn_stats(stats[:, h, j, :], u[:, h, j * P:(j + 1) * P])
                                m.then_inc(sm2["stats"][team], 1)
                            elif name == "mean":
                                dve.wait_ge(sm2["stats"][team], 1)
                                dve.wait_ge(sm2["stats"][team], nth(i, h))
                                for j in range(4):
                                    m = dve.bn_aggr(mv[:, h, j, :], stats[:, h, j, :])
                                m.then_inc(sm2["mv"][team], 1)
                            elif name == "result":
                                dve.wait_ge(sm2["rstd"][team], nth(i, h))
                                dve.wait_ge(stores[h], i * 16 + 16)
                                for j in range(4):
                                    col = slice(j * P, (j + 1) * P)
                                    m = dve.tensor_scalar(res[:, h, col], u[:, h, col], mv[:, h, j, 0:1],
                                                          rstd[:, h, j:j + 1], ALU.subtract, ALU.mult)
                                m.then_inc(sm2["res"][team], 1)
                        if name == "mean":
                            for h in TEAMS[team]:
                                dve.wait_ge(sm2["mv"][team], nth(i, h))
                                dve.tensor_scalar(var[:, h, :], mv[:, h, :, 1], EPS, None, ALU.add
                                                  ).then_inc(sm2["var"][team], 1)

                    dve.wait_ge(w_in, 32)
                    for team in range(2):
                        dve.sem_inc(sm2["res"][team], len(TEAMS[team]))
                    in_turns(dve, STEPS, HALF, step)

                @block.scalar
                def _(act):
                    def step(i, team, name, k, last):
                        if name == "residual" and k == 1:
                            for h in TEAMS[team]:
                                act.wait_ge(loaded[h], i * 48 + 48)
                                act.wait_ge(sm2["res"][team], last_round(i, h))
                                act.activation(gx[:, h, :], xT[:, h, :], ACT.Identity, scale=cols[:, GATE:GATE + 1],
                                               bias=cols[:, BV:BV + 1]).then_inc(sm2["gx"][team], 1)
                        if name != "log":
                            return
                        for h in TEAMS[team]:
                            act.wait_ge(sm2["low"][team], nth(i, h, SOFTS, k))
                            act.activation(low[:, h, :], low[:, h, :], ACT.Exp).then_inc(sm2["ex"][team], 1)
                        for h in TEAMS[team]:
                            act.wait_ge(sm2["ex"][team], nth(i, h, SOFTS, k))
                            act.activation(low[:, h, :], low[:, h, :], ACT.Ln, bias=1.0).then_inc(sm2["ln"][team], 1)

                    act.wait_ge(w_in, 32)
                    act.preload_act_table_set("natural_log_exp_and_others")
                    in_turns(act, STEPS, HALF, step)

                @block.tensor
                def _(pe):
                    def step(i, team, name, k, last):
                        for h in TEAMS[team]:
                            if name == "sum":
                                pe.wait_ge(pair_in[h], i * (16 * ACCS) + 16 * ACCS)
                                pe.wait_ge(sm2["res"][team], last_round(i, h))
                                for j in range(4):
                                    col = slice(j * P, (j + 1) * P)
                                    m = pe.transpose(mm_ps[h][:, col], pair[:, h, col], ident[:, :])
                                m.then_inc(sm2["summed"][team], 1)
                            elif name == "max" and k == 6:
                                pe.wait_ge(sm2["sp"][team], nth(i, h, SOFTS, 6))
                                pe.wait_ge(sm2["gx"][team], nth(i, h))
                                for j in range(4):
                                    col = slice(j * P, (j + 1) * P)
                                    pe.matmul(mm_ps[h][:, col], sp_u[:, h, col], wts[:, WV, :], start=True, stop=False)
                                    m = pe.matmul(mm_ps[h][:, col], gx[:, h, col], ident[:, :], start=False,
                                                  stop=True)
                                m.then_inc(sm2["mm"][team], 1)
                            elif name == "max":
                                w = (W2 if k % 2 else W1) + k // 2
                                pe.wait_ge(sm2["sp"][team], nth(i, h, SOFTS, k))
                                pe.matmul(mm_ps[h][:, :], wts[:, w, :], sp_u[:, h, :], start=True, stop=True
                                          ).then_inc(sm2["mm"][team], 1)

                    pe.wait_ge(w_in, 32)
                    in_turns(pe, STEPS, HALF, step)
            end_stage()


def kernel(x, src, dst, edge_attr_64, edge_weight, L1_gnn_Wg, L1_gnn_Wi, L1_gnn_bi, L1_gnn_Wj, L1_gnn_bj,
           L1_gnn_Wv, L1_gnn_bv, L1_gnn_gate, L1_gnn_res_W1, L1_gnn_res_b1, L1_gnn_res_W2, L1_gnn_res_b2):
    import numpy as np
    import concourse.bacc as bacc
    from concourse.bass_utils import run_bass_kernel_spmd

    n, edges = x.shape[0], src.shape[0]
    chunks, nrows = sizes(n, edges)
    tiles = chunks * CT
    epad = tiles * P - edges

    src = np.concatenate([np.asarray(src), np.full(epad, n, src.dtype)])
    dst = np.concatenate([np.asarray(dst), np.full(epad, n, dst.dtype)])
    attr = np.concatenate([np.asarray(edge_attr_64), np.zeros((epad, R), np.float32)])
    weights = np.concatenate([np.asarray(L1_gnn_Wi)[None], np.asarray(L1_gnn_Wj)[None], np.asarray(L1_gnn_res_W1),
                              np.asarray(L1_gnn_res_W2), np.asarray(L1_gnn_Wv)[None]])
    cols = np.concatenate([np.asarray(L1_gnn_bi)[None], np.asarray(L1_gnn_res_b1), np.asarray(L1_gnn_res_b2),
                           np.asarray(L1_gnn_bv)[None], np.asarray(L1_gnn_gate)[None]])
    arrays = {
        "x": np.concatenate([np.asarray(x), np.zeros((nrows - n, P), np.float32)]),
        "src_col": src.reshape(tiles, P).T, "dst_col": dst.reshape(tiles, P).T,
        "src_row": src.reshape(P, tiles), "dst_row": dst.reshape(P, tiles),
        "attr_t": attr.T,
        "WgT": np.asarray(L1_gnn_Wg).T,
        "WT": weights.transpose(2, 0, 1),
        "cols": cols.T,
        "bj": np.asarray(L1_gnn_bj)[None],
    }
    arrays = {f"in_{k}": np.ascontiguousarray(a) for k, a in arrays.items()}
    nc = bacc.Bacc("TRN2", target_bir_lowering=False, num_devices=1)
    ins = {k[3:]: nc.dram_tensor(k, a.shape, mybir.dt.from_np(a.dtype), kind="ExternalInput").ap()
           for k, a in arrays.items()}
    out = nc.dram_tensor("out_0", [nrows, P], F32, kind="ExternalOutput").ap()
    gnn_kernel(nc, edges, ins, out)
    r = run_bass_kernel_spmd(nc, [arrays], core_ids=[0])
    return r.results[0]["out_0"][:n]
```
